# Optimizing a Trainium2 kernel written in Bass

```python
import numpy as np
import jax
import jax.numpy as jnp

def _softmax(x, axis=-1):
    return jax.nn.softmax(x, axis=axis)

def _gelu(x):
    return jax.nn.gelu(x, approximate=True)

def _silu(x):
    return jax.nn.silu(x)

def _sigmoid(x):
    return jax.nn.sigmoid(x)

def _layernorm(x, axis=-1, eps=1e-05):
    m = jnp.mean(x, axis=axis, keepdims=True)
    v = jnp.var(x, axis=axis, keepdims=True)
    return (x - m) / jnp.sqrt(v + eps)

def _scatter_add(tgt, idx, src, axis=0):
    return tgt.at[idx].add(src)

def _segment_sum(src, seg, n):
    return jax.ops.segment_sum(src, seg, n)
kernel_name = 'mk_conv_seq_d2_conv_nchw128_r2_482877'

def setup_inputs(seed: int=0):
    np.random.seed(seed)
    _w = jnp.asarray

    def _rec_inputs():
        import jax
        import jax.numpy as jnp
        _gk = jax.random.key(seed)
        x = -0.0003929 + 0.9999 * jax.random.normal(jax.random.fold_in(_gk, 1), (8, 64, 64, 64), jnp.float32)
        return x
    x = _rec_inputs()

    def _L0_conv_setup():
        import jax, jax.numpy as jnp
        import numpy as np
        from jax import lax
        B, C, H, W = (8, 64, 64, 64)
        KW = 9
        PW = (KW - 1) // 2

        def _make_kernel(key):
            std = float(np.sqrt(2.0 / (C * KW * C)))
            return jax.random.normal(key, (KW, C, C), dtype=jnp.float32) * std

        def _row_conv(y, K):
            return lax.conv_general_dilated(y, K, window_strides=(1,), padding=[(PW, PW)], dimension_numbers=('NWC', 'WIO', 'NWC'))

        def _dir_scan(x, K, reverse):
            if reverse:
                x = x[:, ::-1]

            def step(prev, cur):
                new = cur + jax.nn.relu(_row_conv(prev, K))
                return (new, new)
            first = x[:, 0]
            _, rest = lax.scan(step, first, jnp.moveaxis(x[:, 1:], 1, 0))
            out = jnp.concatenate([first[:, None], jnp.moveaxis(rest, 0, 1)], axis=1)
            if reverse:
                out = out[:, ::-1]
            return out
        key = jax.random.key(seed)
        kx, k1, k2, k3, k4 = jax.random.split(key, 5)
        x = jax.random.normal(kx, (B, C, H, W), dtype=jnp.float32)
        return {'x': x, 'k_td': _make_kernel(k1), 'k_dt': _make_kernel(k2), 'k_lr': _make_kernel(k3), 'k_rl': _make_kernel(k4)}
    _L0_conv_all = _L0_conv_setup()
    _L0_conv_in = {k: v for k, v in _L0_conv_all.items() if k in ('k_td', 'k_dt', 'k_lr', 'k_rl')}
    del _L0_conv_all

    def _L1_conv_setup():
        import jax, jax.numpy as jnp
        import numpy as np
        EPS_GN = 1e-05
        EPS_ATTN = 1e-06
        HEADS = 4
        DIM_HEAD = 32
        GROUPS = 32

        def group_norm(x, weight, bias, groups=GROUPS, eps=EPS_GN):
            b, c, h, w = x.shape
            xg = x.reshape(b, groups, c // groups, h, w)
            mean = xg.mean(axis=(2, 3, 4), keepdims=True)
            var = xg.var(axis=(2, 3, 4), keepdims=True)
            xg = (xg - mean) * jax.lax.rsqrt(var + eps)
            x = xg.reshape(b, c, h, w)
            return x * weight[None, :, None, None] + bias[None, :, None, None]

        def conv1x1(x, w):
            return jnp.einsum('bchw,oc->bohw', x, w)
        key = jax.random.key(seed)
        ks = jax.random.split(key, 6)
        b, c, h, w = (16, 64, 64, 64)
        inner = HEADS * DIM_HEAD
        x = jax.random.normal(ks[0], (b, c, h, w), dtype=jnp.float32)
        gn1_w = jnp.ones((c,), jnp.float32) + 0.02 * jax.random.normal(ks[1], (c,), jnp.float32)
        gn1_b = 0.02 * jax.random.normal(ks[2], (c,), jnp.float32)
        w_qkv = jax.random.normal(ks[3], (inner * 3, c), jnp.float32) / np.sqrt(c)
        w_out = jax.random.normal(ks[4], (c, inner), jnp.float32) / np.sqrt(inner)
        gn2_w = jnp.ones((c,), jnp.float32) + 0.02 * jax.random.normal(ks[5], (c,), jnp.float32)
        gn2_b = jnp.zeros((c,), jnp.float32)
        return {'x': x, 'gn1_w': gn1_w, 'gn1_b': gn1_b, 'w_qkv': w_qkv, 'w_out': w_out, 'gn2_w': gn2_w, 'gn2_b': gn2_b}
    _L1_conv_all = _L1_conv_setup()
    _L1_conv_in = {k: v for k, v in _L1_conv_all.items() if k in ('gn1_w', 'gn1_b', 'w_qkv', 'w_out', 'gn2_w', 'gn2_b')}
    del _L1_conv_all
    return {'x': x, 'L0_conv_k_td': _L0_conv_in['k_td'], 'L0_conv_k_dt': _L0_conv_in['k_dt'], 'L0_conv_k_lr': _L0_conv_in['k_lr'], 'L0_conv_k_rl': _L0_conv_in['k_rl'], 'L1_conv_gn1_w': _L1_conv_in['gn1_w'], 'L1_conv_gn1_b': _L1_conv_in['gn1_b'], 'L1_conv_w_qkv': _L1_conv_in['w_qkv'], 'L1_conv_w_out': _L1_conv_in['w_out'], 'L1_conv_gn2_w': _L1_conv_in['gn2_w'], 'L1_conv_gn2_b': _L1_conv_in['gn2_b']}

def reference(x, L0_conv_k_td, L0_conv_k_dt, L0_conv_k_lr, L0_conv_k_rl, L1_conv_gn1_w, L1_conv_gn1_b, L1_conv_w_qkv, L1_conv_w_out, L1_conv_gn2_w, L1_conv_gn2_b):
    import jax
    import jax.numpy as jnp

    def _L0_conv_ref(x, k_td, k_dt, k_lr, k_rl):
        import jax, jax.numpy as jnp
        import numpy as np
        from jax import lax
        B, C, H, W = (8, 64, 64, 64)
        KW = 9
        PW = (KW - 1) // 2

        def _make_kernel(key):
            std = float(np.sqrt(2.0 / (C * KW * C)))
            return jax.random.normal(key, (KW, C, C), dtype=jnp.float32) * std

        def _row_conv(y, K):
            return lax.conv_general_dilated(y, K, window_strides=(1,), padding=[(PW, PW)], dimension_numbers=('NWC', 'WIO', 'NWC'))

        def _dir_scan(x, K, reverse):
            if reverse:
                x = x[:, ::-1]

            def step(prev, cur):
                new = cur + jax.nn.relu(_row_conv(prev, K))
                return (new, new)
            first = x[:, 0]
            _, rest = lax.scan(step, first, jnp.moveaxis(x[:, 1:], 1, 0))
            out = jnp.concatenate([first[:, None], jnp.moveaxis(rest, 0, 1)], axis=1)
            if reverse:
                out = out[:, ::-1]
            return out
        y = jnp.transpose(x, (0, 2, 3, 1))
        y = _dir_scan(y, k_td, reverse=False)
        y = _dir_scan(y, k_dt, reverse=True)
        yt = jnp.swapaxes(y, 1, 2)
        yt = _dir_scan(yt, k_lr, reverse=False)
        yt = _dir_scan(yt, k_rl, reverse=True)
        y = jnp.swapaxes(yt, 1, 2)
        return jnp.transpose(y, (0, 3, 1, 2))

    def _L1_conv_ref(x, gn1_w, gn1_b, w_qkv, w_out, gn2_w, gn2_b):
        import jax, jax.numpy as jnp
        import numpy as np
        EPS_GN = 1e-05
        EPS_ATTN = 1e-06
        HEADS = 4
        DIM_HEAD = 32
        GROUPS = 32

        def group_norm(x, weight, bias, groups=GROUPS, eps=EPS_GN):
            b, c, h, w = x.shape
            xg = x.reshape(b, groups, c // groups, h, w)
            mean = xg.mean(axis=(2, 3, 4), keepdims=True)
            var = xg.var(axis=(2, 3, 4), keepdims=True)
            xg = (xg - mean) * jax.lax.rsqrt(var + eps)
            x = xg.reshape(b, c, h, w)
            return x * weight[None, :, None, None] + bias[None, :, None, None]

        def conv1x1(x, w):
            return jnp.einsum('bchw,oc->bohw', x, w)
        b, c, h, w = x.shape
        residual = x
        xn = group_norm(x, gn1_w, gn1_b)
        qkv = conv1x1(xn, w_qkv)
        q, k, v = jnp.split(qkv, 3, axis=1)

        def to_tokens(t):
            return t.reshape(b, HEADS, DIM_HEAD, h * w).transpose(0, 1, 3, 2)
        q, k, v = (to_tokens(q), to_tokens(k), to_tokens(v))
        q = jax.nn.elu(q) + 1.0
        k = jax.nn.elu(k) + 1.0
        k_sum = k.sum(axis=2)
        kv = jnp.einsum('bhnd,bhne->bhde', k, v)
        qk_sum = jnp.einsum('bhnd,bhd->bhn', q, k_sum)
        qkv_out = jnp.einsum('bhnd,bhde->bhne', q, kv)
        out = qkv_out / (qk_sum[..., None] + EPS_ATTN)
        out = out.transpose(0, 1, 3, 2).reshape(b, HEADS * DIM_HEAD, h, w)
        out = conv1x1(out, w_out)
        out = group_norm(out, gn2_w, gn2_b)
        return out + residual

    def _gn(v, G=32, eps=1e-05):
        B_, C_, H_, W_ = v.shape
        g = v.reshape(B_, G, C_ // G, H_, W_)
        m = jnp.mean(g, axis=(2, 3, 4), keepdims=True)
        s = jnp.var(g, axis=(2, 3, 4), keepdims=True)
        return ((g - m) / jnp.sqrt(s + eps)).reshape(v.shape)

    def _ln_c(v, eps=1e-06):
        m = jnp.mean(v, axis=1, keepdims=True)
        s = jnp.var(v, axis=1, keepdims=True)
        return (v - m) / jnp.sqrt(s + eps)

    def _ln_t(v, eps=1e-05):
        m = jnp.mean(v, axis=-1, keepdims=True)
        s = jnp.var(v, axis=-1, keepdims=True)
        return (v - m) / jnp.sqrt(s + eps)

    def _to_tokens(v):
        B_, C_, H_, W_ = v.shape
        return v.reshape(B_, C_, H_ * W_).transpose(0, 2, 1)

    def _from_tokens(t, like):
        B_, C_, H_, W_ = like.shape
        return t.transpose(0, 2, 1).reshape(B_, C_, H_, W_)
    x = _L0_conv_ref(x, L0_conv_k_td, L0_conv_k_dt, L0_conv_k_lr, L0_conv_k_rl)
    x = _L1_conv_ref(x, L1_conv_gn1_w, L1_conv_gn1_b, L1_conv_w_qkv, L1_conv_w_out, L1_conv_gn2_w, L1_conv_gn2_b)
    return x

_drawn_inputs = setup_inputs


def setup_inputs(seed=0):
    import zlib

    import numpy as np

    out = dict(_drawn_inputs(seed))
    spreads = {'L1_conv_gn2_b': (0.0, 0.344)}
    factors = {'L1_conv_gn2_w': 3.7}
    for name, (base, spread) in spreads.items():
        noise = np.random.default_rng([zlib.crc32(name.encode()), seed]).standard_normal(out[name].shape)
        drawn = base * np.exp(spread * noise) if base else spread * noise
        out[name] = jnp.asarray(drawn.astype(out[name].dtype))
    for name, factor in factors.items():
        out[name] = (out[name] * factor).astype(out[name].dtype)
    return out
```

```python
import numpy as np

import concourse.bass as bass
from concourse import mybir
from contextlib import ExitStack

F32 = mybir.dt.float32
ALU = mybir.AluOpType
ACT = mybir.ActivationFunctionType

B, C, H, W = 8, 64, 64, 64
KW = 9
P = 2 * C
J = W // 2
HALO = 2
RJ = J + 2 * HALO
TAPS = 2 * HALO + 1
ROW = B * J
STEPS = H - 1
GROUPS = 2
GB = B // GROUPS
SLOTS = 3
BODY = 9
RAW_ROWS = 7
RAW_SLOTS = 3
RAW_B = RAW_ROWS * W + 2
assert H == W and STEPS % BODY == 0 and STEPS % (RAW_ROWS * RAW_SLOTS) == 0


HEADS, DH = 4, 32
HD = HEADS * DH
assert HD == P
NW = W * J
CHUNK = 512
NCHUNK = NW // CHUNK
UNITS = 2 * NCHUNK
KBANKS = NW // 2 // P
EPS_GN, EPS_ATTN = 1e-5, 1e-6
BLOCKS = STEPS // BODY
SPAN = BODY * J


def constants():
    p = np.arange(P)
    head = p // DH
    group = (p % C) // 2
    return np.concatenate([
        np.eye(P), head[:, None] == head[None, :], (group[:, None] == group[None, :]) / 4.0,
        head[:, None] == np.arange(DH)[None, :]], axis=1).astype(np.float32)


def build(nc, x, k_td, k_dt, k_lr, k_rl, gn1_w, gn1_b, w_qkv, w_out, gn2_w, gn2_b, consts, out):
    with ExitStack() as ctx:
        def sb(name, shape, dt=F32):
            return ctx.enter_context(nc.sbuf_tensor(name, shape, dt))

        def sem(name):
            return ctx.enter_context(nc.semaphore(name))

        ring = sb("ring", [P, SLOTS, B, RJ])
        rows_h = sb("rows_h", [P, H, B, J])
        cols_w = sb("cols_w", [P, W * B * J])
        wts = sb("wts", [P, 4, TAPS, P])
        bank = [ctx.enter_context(nc.psum_tensor(f"bank{n}", [P, 512], F32)) for n in range(8)]
        conv = bank[0:2]
        key_ps, tok_ps, acc_ps, query_ps, small_ps, out_ps = bank[0:2], bank[2], bank[3], bank[4:6], bank[6], bank[7]
        proj_ps = (out_ps, small_ps)
        cols = cols_w[:, :].rearrange("p (w b j) -> p w b j", w=W, b=B)
        raw = cols_w[:, 0:RAW_SLOTS * B * RAW_B].rearrange("p (s b e) -> p s b e", s=RAW_SLOTS, b=B)
        row0 = sb("row0", [P, B, W + 2])
        flat_h = rows_h[:, :, :, :].rearrange("p h b j -> p (h b j)")
        qp = flat_h[:, 0:2 * UNITS * CHUNK].rearrange("p (r u n) -> p r u n", r=2, u=UNITS)
        recip_b = flat_h[:, 2 * UNITS * CHUNK:3 * UNITS * CHUNK].rearrange("p (u n) -> p u n", u=UNITS)
        proj = flat_h[:, 3 * UNITS * CHUNK:3 * UNITS * CHUNK + 2 * NW].rearrange("p (r n) -> p r n", r=2)
        yn = sb("yn", [P, 2, NW])
        tok = sb("tok", [P, 2, 512])
        kp = sb("kp", [P, 4, 512])
        ex = sb("ex", [P, 2, 512])
        re = sb("re", [P, 2, 512])
        fin = sb("fin", [P, J, W])
        cst = sb("cst", [P, 3 * P + DH])
        ident, same_head, group_mean, head_of = (cst[:, 0:P], cst[:, P:2 * P], cst[:, 2 * P:3 * P],
                                                 cst[:, 3 * P:3 * P + DH])
        ones = sb("ones", [P, DH])
        part = sb("part", [P, 1])
        half = sb("half", [P, B])
        wl = sb("wl", [P, 3, 2, C])
        wol = sb("wol", [C, P])
        w_q = sb("w_q", [P, 2, P])
        w_k = sb("w_k", [P, 2, P])
        w_v = sb("w_v", [P, P])
        w_o = sb("w_o", [P, C])
        norm = sb("norm", [P, 4])
        stats = sb("stats", [P, B, BLOCKS, 6])
        agg = sb("agg", [P, B, 2])
        dev = sb("dev", [P, B])
        spread = sb("spread", [P, B])
        scale1 = sb("scale1", [P, B])
        shift1 = sb("shift1", [P, B])
        acc_g = sb("acc_g", [P, P])
        acc_s = sb("acc_s", [P, 2 * P])
        ksum = sb("ksum", [P, 1])
        den_w = sb("den_w", [P, DH])
        kv = sb("kv", [P, P])
        mix = sb("mix", [P, C])
        den = sb("den", [P, CHUNK])
        recip = sb("recip", [P, 2, CHUNK])
        stats2 = sb("stats2", [P, NCHUNK, 6])
        agg2 = sb("agg2", [P, 2])
        dev2 = sb("dev2", [P, 4])
        scale2 = sb("scale2", [P, 2])
        shift2 = sb("shift2", [P, 2])

        zeroed = sem("zeroed")
        wts_loaded = [sem(f"wts_loaded{k}") for k in range(4)]
        row0_loaded = sem("row0_loaded")
        raw_loaded = [sem(f"raw_loaded{s}") for s in range(RAW_SLOTS)]
        row_ready = [sem(f"row_ready{g}") for g in range(GROUPS)]
        conv_done = [sem(f"conv_done{g}") for g in range(GROUPS)]
        saved = sem("saved")
        stored = sem("stored")
        consts_loaded, norm_loaded, proj_loaded = sem("consts_loaded"), sem("norm_loaded"), sem("proj_loaded")
        wt_done, wt_ready = sem("wt_done"), sem("wt_ready")
        stat_ready, stat_done = sem("stat_ready"), sem("stat_done")
        chain = sem("chain")
        yn_ready, tok_done, tok_ready = sem("yn_ready"), sem("tok_done"), sem("tok_ready")
        key_done, key_read, kp_ready, acc_used = sem("key_done"), sem("key_read"), sem("kp_ready"), sem("acc_used")
        query_done, query_read, qp_ready = sem("query_done"), sem("query_read"), sem("qp_ready")
        acc_read, small_done, small_read = sem("acc_read"), sem("small_done"), sem("small_read")
        recip_ready, normed, norm2 = sem("recip_ready"), sem("normed"), sem("norm2")
        passed = sem("passed")
        var_ready, scale_ready = sem("var_ready"), sem("scale_ready")
        recip_sent = [sem(f"recip_sent{m}") for m in range(2)]
        proj_done, proj_read = sem("proj_done"), sem("proj_read")
        affine_ready, affine_done, fin_ready = sem("affine_ready"), sem("affine_done"), sem("fin_ready")

        def at_least(eng, s, n):
            if not isinstance(n, int) or n > 0:
                eng.wait_ge(s, n)

        def settled(eng):
            eng.sem_inc(passed, 1)

        def batches(eng, body):
            for b in (0, 1):
                body(b, b % 2, True, b >= 1, False)
            with eng.Fori(0, (B - 2) // 2) as n:
                for i in range(2):
                    body(n * 2 + (2 + i), i, True, True, True)
            body(B, 0, False, True, True)
            body(B + 1, 1, False, False, True)

        def spread_heads(src):
            return bass.AP(tensor=src.tensor, offset=src.offset, ap=[src.ap[0], [0, DH], [1, CHUNK]])

        block = ctx.enter_context(nc.Block())

        @block.sync
        def _(sp):
            def load_weights(s, k):
                for pi, po, tap, pair in ((0, 0, 0, 0), (1, 1, 0, 0), (1, 0, 1, 0), (0, 1, 1, 1)):
                    n = TAPS - tap
                    sp.dma_start(wts[pi * C:(pi + 1) * C, s, pair:pair + n, po * C:(po + 1) * C],
                                 k[tap:KW:2, :, :].rearrange("t i o -> i t o")).then_inc(wts_loaded[s], 16)

            sp.dma_start(row0[0:C, :, 1:1 + W], x[:, :, 0, :].rearrange("b c w -> c b w")).then_inc(row0_loaded, 16)
            sp.dma_start(row0[C:P, :, 0:W], x[:, :, 0, :].rearrange("b c w -> c b w")).then_inc(row0_loaded, 16)
            sp.wait_ge(zeroed, 2)
            load_weights(0, k_td)
            for n in range(STEPS // RAW_ROWS):
                s = n % RAW_SLOTS
                h0 = 1 + n * RAW_ROWS
                if n >= RAW_SLOTS:
                    for g in range(GROUPS):
                        sp.wait_ge(row_ready[g], 1 + (n - RAW_SLOTS + 1) * RAW_ROWS)
                for half in range(2):
                    sp.dma_start(raw[half * C:(half + 1) * C, s, :, 1 - half:1 - half + RAW_ROWS * W],
                                 x[:, :, h0:h0 + RAW_ROWS, :].rearrange("b c h w -> c b (h w)"))\
                      .then_inc(raw_loaded[s], 16)
                if n == 1:
                    for s_, k in ((1, k_dt), (2, k_lr), (3, k_rl)):
                        load_weights(s_, k)
            sp.dma_start(cst[:, :], consts).then_inc(consts_loaded, 16)
            for d in range(2):
                sp.dma_start(wl[:, :, d, :], w_qkv.rearrange("(t o) c -> o t c", t=3)).then_inc(proj_loaded, 16)
            sp.dma_start(wol[:, :], w_out).then_inc(proj_loaded, 16)
            for n, v in enumerate((gn1_w, gn1_b, gn2_w, gn2_b)):
                for d in range(2):
                    sp.dma_start(norm[d * C:(d + 1) * C, n:n + 1], v.rearrange("(c a) -> c a", a=1))\
                      .then_inc(norm_loaded, 16)

            def tail(b, par, cur, prev, pp):
                if prev:
                    for m in range(2):
                        at_least(sp, recip_ready, 2 * (b - 1) + m + 1)
                        settled(sp)
                        at_least(sp, normed, UNITS * (b - 1))
                        for u in range(4):
                            src = recip[DH * u:DH * u + HEADS, m, :]
                            sp.dma_start(recip_b[:, 4 * m + u, :], spread_heads(src)).then_inc(recip_sent[m], 16)
                if pp:
                    at_least(sp, fin_ready, b - 1)
                    for d in range(2):
                        dst = out[bass.ds(b - 2, 1), :, :, :] if not isinstance(b, int) else out[b - 2:b - 1]
                        dst = dst.rearrange("o c (j d) w -> d (o c) j w", d=2)[d]
                        sp.dma_start(dst, fin[d * C:(d + 1) * C, :, :]).then_inc(stored, 16)

            batches(sp, tail)
            sp.wait_ge(stored, 32 * B)

        @block.gpsimd
        def _(pool):
            nc.gpsimd.memset(wts[:, :, TAPS - 1, 0:C], 0.0)
            nc.gpsimd.memset(wts[:, :, 0, C:P], 0.0).then_inc(zeroed, 1)
            nc.gpsimd.memset(ring[:], 0.0).then_inc(zeroed, 1)
            nc.gpsimd.memset(w_q[:], 0.0)
            nc.gpsimd.memset(ones[:], 1.0)
            nc.gpsimd.memset(part[:], 1.0 / DH)
            nc.gpsimd.memset(half[:], -0.5)
            nc.gpsimd.memset(w_k[:], 0.0).then_inc(zeroed, 1)

            pool.wait_ge(var_ready, 1)
            nc.gpsimd.tensor_tensor(scale1[:, :], dev[:, :], half[:, :], ALU.pow).then_inc(scale_ready, 1)
            pool.wait_ge(scale_ready, 1)
            nc.gpsimd.tensor_scalar(scale1[:, :], scale1[:, :], norm[:, 0:1], None, ALU.mult).then_inc(scale_ready, 1)

            def tail(b, par, cur, prev, pp):
                if pp:
                    at_least(pool, small_read, 4 * (b - 1) + 2)
                    nc.gpsimd.tensor_tensor(scale2[:, par:par + 1], dev2[:, 1:2], half[:, 0:1], ALU.pow)\
                        .then_inc(scale_ready, 1)
                    at_least(pool, scale_ready, 2 * b - 1)
                    settled(pool)
                    nc.gpsimd.tensor_scalar(scale2[:, par:par + 1], scale2[:, par:par + 1], norm[:, 2:3], None,
                                            ALU.mult).then_inc(scale_ready, 1)
                    at_least(pool, scale_ready, 2 * b)
                    settled(pool)
                    nc.gpsimd.tensor_scalar(shift2[:, par:par + 1], dev2[:, 3:4], scale2[:, par:par + 1],
                                            norm[:, 3:4], ALU.mult, ALU.add).then_inc(affine_ready, 1)
                    at_least(pool, affine_done, b - 1)
                    at_least(pool, stored, 32 * (b - 2))
                    nc.gpsimd.tensor_tensor(
                        fin[:, :, :].rearrange("p j w -> p w j"),
                        proj[:, par, :].rearrange("p (w j) -> p w j", j=J),
                        cols[:, :, bass.ds(b - 2, 1), :].rearrange("p w o j -> p w (o j)"), ALU.add)\
                        .then_inc(fin_ready, 1)
                if prev:
                    for u in range(UNITS):
                        if u % 4 == 0:
                            at_least(pool, recip_sent[u // 4], 64 * b)
                        nc.gpsimd.tensor_tensor(qp[:, 1 - par, u, :], qp[:, 1 - par, u, :], recip_b[:, u, :],
                                                ALU.mult).then_inc(normed, 1)

            batches(pool, tail)

        @block.tensor
        def _(pe):
            pe.wait_ge(zeroed, 2)
            for k in range(4):
                if k == 1:
                    pe.wait_ge(zeroed, 3)
                    pe.wait_ge(consts_loaded, 16)
                    pe.wait_ge(proj_loaded, 48)
                    for n in range(3):
                        nc.tensor.transpose(tok_ps[:, n * P:(n + 1) * P], wl[:, n].rearrange("p d c -> p (d c)"), ident)
                    nc.tensor.transpose(acc_ps[:, 0:C], wol[:, :], cst[0:C, 0:C]).then_inc(wt_done, 1)
                rows = (1, 64, 128, 191)[k]
                pe.wait_ge(wts_loaded[k], 64)
                with pe.Fori(0, STEPS - BODY + 1, BODY) as s:
                    for u in range(BODY):
                        for g in range(GROUPS):
                            pe.wait_ge(row_ready[g], s + (rows + u))
                            for d in range(TAPS):
                                last = nc.tensor.matmul(conv[g][:, 0:GB * J], wts[:, k, d, :],
                                                        ring[:, u % SLOTS, g * GB:(g + 1) * GB, d:d + J],
                                                        start=d == 0, stop=d == TAPS - 1)
                            last.then_inc(conv_done[g], 1)

            pe.wait_ge(wt_ready, 1)
            for n, v in enumerate((agg[:, :, 0], spread[:, :])):
                pe.wait_ge(stat_ready, n + 1)
                nc.tensor.matmul(small_ps[:, n * B:(n + 1) * B], group_mean, v, start=True, stop=True)\
                    .then_inc(stat_done, 1)

            def keys(b, par, i):
                at_least(pe, yn_ready, b + 1)
                at_least(pe, tok_ready, 4 * b + i)
                for n in range(4):
                    t = nc.tensor.transpose(tok_ps[:, n * P:(n + 1) * P], yn[:, par, (4 * i + n) * P:(4 * i + n + 1) * P],
                                            ident)
                t.then_inc(tok_done, 1)
                for m in (2 * i, 2 * i + 1):
                    at_least(pe, key_read, KBANKS * b + m - 1)
                    for n in range(2):
                        at = (2 * m + n) * P
                        k = nc.tensor.matmul(key_ps[m % 2][:, n * 2 * P:(n + 1) * 2 * P], yn[:, par, at:at + P],
                                             w_k[:, :, :].rearrange("p d n -> p (d n)"), start=True, stop=True)
                    k.then_inc(key_done, 1)

            def queries(b, par, i):
                for d in range(2):
                    u = 2 * i + d
                    at_least(pe, query_read, UNITS * b + u - 1)
                    nc.tensor.matmul(query_ps[d][:, :], w_q[:, d, :], yn[:, par, i * CHUNK:(i + 1) * CHUNK],
                                     start=True, stop=True).then_inc(query_done, 1)

            def gather(b, i):
                at_least(pe, kp_ready, KBANKS * b + 2 * i + 2)
                at_least(pe, tok_ready, 4 * b + i + 1)
                if i == 0:
                    at_least(pe, acc_read, b)
                for n in range(4):
                    for d in range(2):
                        nc.tensor.matmul(acc_ps[d * C:(d + 1) * C, 0:P], tok[:, i % 2, n * P + d * C:n * P + (d + 1) * C],
                                         kp[:, (2 * i + n // 2) % 4, (n % 2) * 2 * P + d * P:(n % 2) * 2 * P + (d + 1) * P],
                                         start=i == 0 and n == 0, stop=i == 3 and n == 3, skip_group_check=True)
                for n in range(4):
                    last = nc.tensor.matmul(acc_ps[DH * n:DH * (n + 1), P:3 * P], ones[:, :],
                                            kp[:, (2 * i + n // 2) % 4, (n % 2) * 2 * P:(n % 2 + 1) * 2 * P],
                                            start=False, stop=i == 3, skip_group_check=True)
                last.then_inc(acc_used, 1)

            def small(b, n, prev, pp):
                at_least(pe, small_read, 4 * (b - 1) + n)
                if n == 0:
                    at_least(pe, proj_read, NCHUNK * (b - 1))
                    if prev:
                        at_least(pe, acc_read, b)
                        for d in range(2):
                            last = nc.tensor.matmul(small_ps[:, 0:1], acc_s[:, d * P:(d + 1) * P], part[:, :],
                                                    start=d == 0, stop=d == 1)
                        last = nc.tensor.matmul(small_ps[:, P:2 * P], w_v[:, :], acc_g[:, :], start=True, stop=True)
                    if pp:
                        at_least(pe, stat_ready, 2 * (b - 2) + 3)
                        last = nc.tensor.matmul(small_ps[:, 2 * P:2 * P + 1], group_mean, agg2[:, 0:1],
                                                start=True, stop=True)
                if n == 1:
                    if prev:
                        last = nc.tensor.matmul(small_ps[:, 0:C], kv[:, :], w_o[:, :], start=True, stop=True)
                    if pp:
                        at_least(pe, stat_ready, 2 * (b - 2) + 4)
                        last = nc.tensor.matmul(small_ps[:, 2 * P:2 * P + 1], group_mean, dev2[:, 2:3],
                                                start=True, stop=True)
                last.then_inc(small_done, 1)

            def denominators(b, par, m):
                at_least(pe, small_read, 4 * (b - 1) + 2 + m)
                at_least(pe, qp_ready, UNITS * (b - 1) + 4 * m + 4)
                for u in range(4):
                    last = nc.tensor.matmul(small_ps[DH * u:DH * (u + 1), :], den_w[:, :], qp[:, 1 - par, 4 * m + u, :],
                                            start=True, stop=True)
                last.then_inc(small_done, 1)

            def outputs(b, par, chunks):
                for i in chunks:
                    at_least(pe, small_read, 4 * b)
                    at_least(pe, proj_read, NCHUNK * (b - 1) + i - 1)
                    at_least(pe, normed, UNITS * (b - 1) + 2 * i + 2)
                    for d in range(2):
                        last = nc.tensor.matmul(proj_ps[i % 2][d * C:(d + 1) * C, :], mix[:, :],
                                                qp[:, 1 - par, 2 * i + d, :], start=True, stop=True)
                    last.then_inc(proj_done, 1)

            def tail(b, par, cur, prev, pp):
                for i in range(4):
                    if cur:
                        keys(b, par, i)
                    if i == 0 and prev:
                        gather(b - 1, 3)
                    if i == 1 and (prev or pp):
                        small(b, 1, prev, pp)
                    if i == 2 and prev:
                        denominators(b, par, 1)
                    if i == 3 and prev:
                        outputs(b, par, (0, 1))
                    if cur:
                        queries(b, par, i)
                        if i > 0:
                            gather(b, i - 1)
                    if i == 0 and (prev or pp):
                        small(b, 0, prev, pp)
                    if i == 1 and prev:
                        denominators(b, par, 0)
                if prev:
                    outputs(b, par, (2, 3))

            batches(pe, tail)

        @block.vector
        def _(dve):
            dve.wait_ge(row0_loaded, 32)
            dve.wait_ge(zeroed, 2)
            for g in range(GROUPS):
                nc.vector.tensor_copy(ring[:, 0, g * GB:(g + 1) * GB, HALO:HALO + J],
                                      row0[:, g * GB:(g + 1) * GB, 1:1 + W:2]).then_inc(row_ready[g], 1)

            def step(u, g, add):
                return nc.vector.scalar_tensor_tensor(
                    out=ring[:, (u + 1) % SLOTS, g * GB:(g + 1) * GB, HALO:HALO + J],
                    in0=conv[g][:, 0:GB * J].rearrange("p (b j) -> p b j", b=GB), scalar=0.0, in1=add,
                    op0=ALU.max, op1=ALU.add).then_inc(row_ready[g], 1)

            for k in range(4):
                base = k * STEPS
                save = (1, 65, 128, 191)[k]
                if k == 2:
                    dve.wait_ge(saved, 128)
                    for g in range(GROUPS):
                        nc.vector.tensor_copy(ring[:, 0, g * GB:(g + 1) * GB, HALO:HALO + J],
                                              cols[:, 0, g * GB:(g + 1) * GB, :]).then_inc(row_ready[g], 1)
                body = RAW_ROWS * RAW_SLOTS if k == 0 else BODY

                def steps(n, stat=None):
                    s = n * body
                    down = n * -body + (H - 2)
                    for u in range(body):
                        if k == 0 and u % RAW_ROWS == 0:
                            dve.wait_ge(raw_loaded[u // RAW_ROWS], n * 32 + 32)
                        dve.wait_ge(saved, s + (save + u))
                        for g in range(GROUPS):
                            gb = slice(g * GB, (g + 1) * GB)
                            if k == 0:
                                r = u % RAW_ROWS
                                add = raw[:, u // RAW_ROWS, gb, 1 + r * W:1 + (r + 1) * W:2]
                            elif k == 2:
                                add = cols[:, bass.ds(s + (u + 1), 1), gb, :].rearrange("p o b j -> p (o b) j")
                            else:
                                src = rows_h if k == 1 else cols
                                add = src[:, bass.ds(down - u, 1), gb, :].rearrange("p o b j -> p (o b) j")
                            dve.wait_ge(conv_done[g], s + (base + u + 1))
                            step(u, g, add)
                        if stat is not None and u < B:
                            stat(u)

                if k < 3:
                    with dve.Fori(0, STEPS // body) as n:
                        steps(n)
                else:
                    steps(0)
                    with dve.Fori(1, BLOCKS) as n:
                        steps(n, lambda b: nc.vector.bn_stats(
                            stats[:, b, bass.ds(n - 1, 1), :].rearrange("p o s -> p (o s)"),
                            cols[:, bass.ds(W - n * BODY, BODY), b, :]))
                if k == 0:
                    dve.wait_ge(wt_done, 1)
                    for n, w in ((0, w_q), (1, w_k)):
                        for d in range(2):
                            nc.vector.tensor_copy(w[d * C:(d + 1) * C, d, :], tok_ps[d * C:(d + 1) * C, n * P:(n + 1) * P])
                    nc.vector.tensor_copy(w_v[:, :], tok_ps[:, 2 * P:3 * P])
                    nc.vector.tensor_copy(w_o[:, :], acc_ps[:, 0:C]).then_inc(wt_ready, 1)

            def link(ins, count):
                ins.then_inc(chain, 1)
                dve.wait_ge(chain, count)

            dve.wait_ge(saved, 254)
            dve.wait_ge(norm_loaded, 16 * 8)
            for b in range(B):
                last = nc.vector.bn_stats(stats[:, b, BLOCKS - 1, :], cols[:, 0:W - (BLOCKS - 1) * BODY, b, :])
            link(last, 1)
            for b in range(B):
                last = nc.vector.bn_aggr(agg[:, b, :], stats[:, b, :, :].rearrange("p n s -> p (n s)"))
            last.then_inc(stat_ready, 1)
            dve.wait_ge(stat_ready, 1)
            dve.wait_ge(stat_done, 1)
            mean1, var1 = small_ps[:, 0:B], small_ps[:, B:2 * B]
            link(nc.vector.scalar_tensor_tensor(out=dev[:, :], in0=mean1, scalar=-1.0, in1=agg[:, :, 0],
                                                op0=ALU.mult, op1=ALU.add), 2)
            link(nc.vector.tensor_tensor(dev[:, :], dev[:, :], dev[:, :], ALU.mult), 3)
            nc.vector.tensor_tensor(spread[:, :], dev[:, :], agg[:, :, 1], ALU.add).then_inc(stat_ready, 1)
            dve.wait_ge(stat_done, 2)
            nc.vector.tensor_scalar(dev[:, :], var1, EPS_GN, None, ALU.add).then_inc(var_ready, 1)
            dve.wait_ge(scale_ready, 2)
            link(nc.vector.scalar_tensor_tensor(out=shift1[:, :], in0=mean1, scalar=-1.0, in1=scale1[:, :],
                                                op0=ALU.mult, op1=ALU.mult), 4)
            link(nc.vector.tensor_scalar(shift1[:, :], shift1[:, :], norm[:, 1:2], None, ALU.add), 5)

            def normalise(b, par):
                at_least(dve, query_done, UNITS * (b - 1))
                one = lambda v: v[:, bass.ds(b, 1)]
                nc.vector.tensor_scalar(yn[:, par, :].rearrange("p (w j) -> p w j", j=J),
                                        cols[:, :, bass.ds(b, 1), :].rearrange("p w o j -> p w (o j)"),
                                        one(scale1), one(shift1), ALU.mult, ALU.add).then_inc(yn_ready, 1)

            def tokens(b, i):
                at_least(dve, tok_done, 4 * b + i + 1)
                at_least(dve, acc_used, 4 * b + i - 1)
                nc.vector.tensor_copy(tok[:, i % 2, :], tok_ps[:, :]).then_inc(tok_ready, 1)

            def elu1(out_, slot):
                return nc.vector.scalar_tensor_tensor(out=out_, in0=ex[:, slot, :], scalar=1.0, in1=re[:, slot, :],
                                                      op0=ALU.min, op1=ALU.add)

            def keys(b, i):
                for m in (2 * i, 2 * i + 1):
                    at_least(dve, key_read, KBANKS * b + m + 1)
                    at_least(dve, acc_used, 4 * b + m // 2 - 1)
                    elu1(kp[:, m % 4, :], m % 2).then_inc(kp_ready, 1)

            def queries(b, par, i):
                for u in (2 * i, 2 * i + 1):
                    at_least(dve, query_read, UNITS * b + u + 1)
                    at_least(dve, proj_done, NCHUNK * (b - 1))
                    elu1(qp[:, par, u, :], u % 2).then_inc(qp_ready, 1)

            def gathered(b):
                at_least(dve, acc_used, 4 * b)
                at_least(dve, small_read, 4 * (b - 1))
                nc.vector.tensor_copy(acc_g[:, :], acc_ps[:, 0:P])
                nc.vector.tensor_copy(acc_s[:, :], acc_ps[:, P:3 * P]).then_inc(acc_read, 1)

            def small(b, par, n, prev, pp):
                c = b - 2
                mean2 = small_ps[:, 2 * P:2 * P + 1]
                at_least(dve, small_done, 4 * (b - 1) + n + 1)
                if n == 0:
                    if prev:
                        at_least(dve, small_read, 4 * (b - 1))
                        nc.vector.tensor_scalar(den_w[:, :], head_of, small_ps[:, 0:1], None, ALU.mult)
                        last = nc.vector.tensor_tensor(kv[:, :], small_ps[:, P:2 * P], same_head, ALU.mult)
                    if pp:
                        nc.vector.tensor_scalar(dev2[:, 3:4], mean2, -1.0, None, ALU.mult)
                        at_least(dve, stat_ready, 2 * c + 3)
                        last = nc.vector.scalar_tensor_tensor(out=dev2[:, 0:1], in0=mean2, scalar=-1.0,
                                                              in1=agg2[:, 0:1], op0=ALU.mult, op1=ALU.add)
                    last.then_inc(small_read, 1)
                    if pp:
                        at_least(dve, small_read, 4 * (b - 1) + 1)
                        nc.vector.tensor_scalar(dev2[:, 2:3], dev2[:, 0:1], dev2[:, 0:1], agg2[:, 1:2],
                                                ALU.mult, ALU.add).then_inc(stat_ready, 1)
                if n == 1:
                    if prev:
                        last = nc.vector.tensor_copy(mix[:, :], small_ps[:, 0:C])
                    if pp:
                        last = nc.vector.tensor_scalar(dev2[:, 1:2], mean2, EPS_GN, None, ALU.add)
                    last.then_inc(small_read, 1)
                if n >= 2:
                    m = n - 2
                    at_least(dve, recip_ready, 2 * (b - 1) + m)
                    nc.vector.tensor_scalar(den[:, :], small_ps[:, :], EPS_ATTN, None, ALU.add).then_inc(small_read, 1)
                    at_least(dve, small_read, 4 * (b - 1) + n + 1)
                    at_least(dve, recip_sent[m], 64 * (b - 1))
                    nc.vector.reciprocal(recip[:, m, :], den[:, :]).then_inc(recip_ready, 1)

            def tail(b, par, cur, prev, pp):
                if cur:
                    normalise(b, par)
                if pp:
                    at_least(dve, proj_read, NCHUNK * (b - 1))
                    for i in range(NCHUNK):
                        last = nc.vector.bn_stats(stats2[:, i, :], proj[:, par, i * CHUNK:(i + 1) * CHUNK])
                    last.then_inc(norm2, 1)
                    at_least(dve, norm2, b - 1)
                    settled(dve)
                    nc.vector.bn_aggr(agg2[:, :], stats2[:, :, :].rearrange("p n s -> p (n s)")).then_inc(stat_ready, 1)
                for i in range(4):
                    if cur:
                        tokens(b, i)
                    if i == 1 and (prev or pp):
                        small(b, par, 0, prev, pp)
                    if i == 2 and prev:
                        small(b, par, 2, prev, pp)
                    if cur:
                        keys(b, i)
                    if i == 0 and prev:
                        gathered(b)
                    if i == 1 and (prev or pp):
                        small(b, par, 1, prev, pp)
                    if i == 2 and prev:
                        small(b, par, 3, prev, pp)
                    if cur:
                        queries(b, par, i)

            batches(dve, tail)

        @block.scalar
        def _(act):
            def wait_rows(n):
                for g in range(GROUPS):
                    act.wait_ge(row_ready[g], n)

            def save(slot, to):
                act.activation(to, ring[:, slot, :, HALO:HALO + J], ACT.Copy).then_inc(saved, 1)

            def scatter(slot, ph, jh, s=None):
                for pw in range(2):
                    dst = cols_w[ph * C:(ph + 1) * C, :].rearrange("p (w two b j) -> p w two b j", two=2, b=B, j=J)
                    dst = dst[:, :, pw, :, bass.ds(jh, 1)].rearrange("p w b o -> p (o b) w")
                    last = act.activation(dst, ring[pw * C:(pw + 1) * C, slot, :, HALO:HALO + J], ACT.Copy)
                last.then_inc(saved, 1)

            wait_rows(1)
            save(0, rows_h[:, 0])
            with act.Fori(0, STEPS - BODY + 1, BODY) as s:
                for u in range(BODY):
                    wait_rows(s + (u + 2))
                    save((u + 1) % SLOTS, rows_h[:, bass.ds(s + (u + 1), 1), :, :].rearrange("p o b j -> p (o b) j"))
            scatter(0, 1, J - 1)
            with act.Fori(0, STEPS // 6) as n:
                for u in range(6):
                    wait_rows(n * 6 + (65 + u))
                    scatter((u + 1) % SLOTS, u % 2, n * -3 + (H // 2 - 1 - (u + 1) // 2))
            for s in range(STEPS - STEPS % 6, STEPS):
                h = H - 2 - s
                wait_rows(65 + s)
                scatter((s + 1) % SLOTS, h % 2, h // 2)
            for k, rows in ((2, 129), (3, 192)):
                with act.Fori(0, STEPS // BODY) as n:
                    for u in range(BODY):
                        wait_rows(n * BODY + (rows + u))
                        w = n * BODY + (u + 1) if k == 2 else n * -BODY + (W - 2 - u)
                        save((u + 1) % SLOTS, cols[:, bass.ds(w, 1), :, :].rearrange("p o b j -> p (o b) j"))

            def elu_parts(ps, slot, read):
                act.activation(ex[:, slot, :], ps, ACT.Exp)
                act.activation(re[:, slot, :], ps, ACT.Relu).then_inc(read, 1)

            def collect(b, par, chunks):
                for i in chunks:
                    at_least(act, proj_done, NCHUNK * (b - 1) + i + 1)
                    at_least(act, fin_ready, b - 2)
                    act.activation(proj[:, 1 - par, i * CHUNK:(i + 1) * CHUNK], proj_ps[i % 2][:, :], ACT.Copy)\
                       .then_inc(proj_read, 1)

            def tail(b, par, cur, prev, pp):
                for i in range(4):
                    if cur:
                        for m in (2 * i, 2 * i + 1):
                            at_least(act, key_done, KBANKS * b + m + 1)
                            at_least(act, qp_ready, UNITS * b + m - 1)
                            elu_parts(key_ps[m % 2][:, :], m % 2, key_read)
                    if i == 2 and pp:
                        at_least(act, affine_ready, b - 1)
                        act.activation(proj[:, par, :], proj[:, par, :], ACT.Identity, bias=shift2[:, par:par + 1],
                                       scale=scale2[:, par:par + 1]).then_inc(affine_done, 1)
                    if i == 3 and prev:
                        collect(b, par, (0, 1))
                    if cur:
                        for u in (2 * i, 2 * i + 1):
                            at_least(act, query_done, UNITS * b + u + 1)
                            at_least(act, kp_ready, KBANKS * b + u + 1)
                            elu_parts(query_ps[u % 2][:, :], u % 2, query_read)
                if prev:
                    collect(b, par, (2, 3))

            batches(act, tail)


_INS = ["x", "L0_conv_k_td", "L0_conv_k_dt", "L0_conv_k_lr", "L0_conv_k_rl", "L1_conv_gn1_w", "L1_conv_gn1_b",
        "L1_conv_w_qkv", "L1_conv_w_out", "L1_conv_gn2_w", "L1_conv_gn2_b"]


def kernel(**inputs):
    import concourse.bacc as bacc
    from concourse.bass_utils import run_bass_kernel_spmd

    nc = bacc.Bacc("TRN2", target_bir_lowering=False, num_devices=1)
    arrays = {name: np.ascontiguousarray(inputs[name]) for name in _INS}
    arrays["consts"] = constants()
    args = [nc.dram_tensor(name, a.shape, mybir.dt.from_np(a.dtype), kind="ExternalInput").ap()
            for name, a in arrays.items()]
    args.append(nc.dram_tensor("out", (B, C, H, W), F32, kind="ExternalOutput").ap())
    build(nc, *args)
    r = run_bass_kernel_spmd(nc, [arrays], core_ids=[0])
    return r.results[0]["out"]
```

```python
import numpy as np

import concourse.bass as bass
from concourse import mybir
from contextlib import ExitStack

F32 = mybir.dt.float32
F16 = mybir.dt.float16
ALU = mybir.AluOpType
ACT = mybir.ActivationFunctionType

B, C, H, W = 8, 64, 64, 64
KW = 9
P = 2 * C
J = W // 2
HALO = 2
RJ = J + 2 * HALO
TAPS = 2 * HALO + 1
ROW = B * J
STEPS = H - 1
GROUPS = 2
GB = B // GROUPS
SLOTS = 3
LOW_SCALE = 256.0
BODY = 9
RAW_ROWS = 7
RAW_SLOTS = 3
RAW_B = RAW_ROWS * W + 2
assert H == W and STEPS % BODY == 0 and STEPS % (RAW_ROWS * RAW_SLOTS) == 0


HEADS, DH = 4, 32
HD = HEADS * DH
assert HD == P
NW = W * J
CHUNK = 512
NCHUNK = NW // CHUNK
UNITS = 2 * NCHUNK
KBANKS = NW // 2 // P
EPS_GN, EPS_ATTN = 1e-5, 1e-6
SUBS = 4
SUB = CHUNK // SUBS
BLOCKS = STEPS // BODY
SPAN = BODY * J


def constants():
    p = np.arange(P)
    head = p // DH
    group = (p % C) // 2
    row = np.arange(SUBS * DH)
    places = SUBS * head[:, None] + (row // DH)[None, :] == (row % DH)[None, :]
    return np.concatenate([np.eye(P), head[:, None] == head[None, :], (group[:, None] == group[None, :]) / 4.0,
                           places], axis=1).astype(np.float32)


def build(nc, x, k_td, k_dt, k_lr, k_rl, gn1_w, gn1_b, w_qkv, w_out, gn2_w, gn2_b, consts, out):
    with ExitStack() as ctx:
        def sb(name, shape, dt=F32):
            return ctx.enter_context(nc.sbuf_tensor(name, shape, dt))

        def sem(name):
            return ctx.enter_context(nc.semaphore(name))

        state = sb("state", [P, SLOTS, B, J])
        high = sb("high", [P, SLOTS, B, RJ], F16)
        low = sb("low", [P, SLOTS, B, RJ], F16)
        high_down = sb("high_down", [P, SLOTS, B, RJ], F16)
        rows_h = sb("rows_h", [P, H, B, J])
        cols_w = sb("cols_w", [P, W * B * J])
        w_high = sb("w_high", [P, 4, TAPS, P], F16)
        w_low = sb("w_low", [P, 4, TAPS, P], F16)
        bank = [ctx.enter_context(nc.psum_tensor(f"bank{n}", [P, 512], F32)) for n in range(8)]
        conv = ((bank[0], bank[4], bank[6]), (bank[1], bank[5], bank[7]))
        key_ps, tok_ps, acc_ps, query_ps, small_ps, out_ps = bank[0:2], bank[2], bank[3], bank[4:6], bank[6], bank[7]
        proj_ps = (out_ps, small_ps)
        cols = cols_w[:, :].rearrange("p (w b j) -> p w b j", w=W, b=B)
        raw = cols_w[:, 0:RAW_SLOTS * B * RAW_B].rearrange("p (s b e) -> p s b e", s=RAW_SLOTS, b=B)
        row0 = sb("row0", [P, B, W + 2])
        flat_h = rows_h[:, :, :, :].rearrange("p h b j -> p (h b j)")
        qp = flat_h[:, 0:2 * UNITS * CHUNK].rearrange("p (r u n) -> p r u n", r=2, u=UNITS)
        recip_b = flat_h[:, 2 * UNITS * CHUNK:3 * UNITS * CHUNK].rearrange("p (u n) -> p u n", u=UNITS)
        proj = flat_h[:, 3 * UNITS * CHUNK:3 * UNITS * CHUNK + 2 * NW].rearrange("p (r n) -> p r n", r=2)
        yn = sb("yn", [P, 2, NW])
        wts = yn[:, :, :].rearrange("p r n -> p (r n)")[:, 0:4 * TAPS * P].rearrange("p (s t n) -> p s t n", s=4, t=TAPS)
        tok = sb("tok", [P, 2, 512])
        kp = sb("kp", [P, 4, 512])
        ex = sb("ex", [P, 2, 512])
        re = sb("re", [P, 2, 512])
        fin = sb("fin", [P, J, W])
        cst = sb("cst", [P, 3 * P + SUBS * DH])
        ident, same_head, group_mean, head_of = (cst[:, 0:P], cst[:, P:2 * P], cst[:, 2 * P:3 * P],
                                                 cst[:, 3 * P:3 * P + SUBS * DH])
        ones = sb("ones", [P, DH])
        part = sb("part", [P, 1])
        half = sb("half", [P, B])
        wl = sb("wl", [P, 3, 2, C])
        wol = sb("wol", [C, P])
        w_q = sb("w_q", [P, 2, P])
        w_k = sb("w_k", [P, 2, P])
        w_v = sb("w_v", [P, P])
        w_o = sb("w_o", [P, C])
        norm = sb("norm", [P, 4])
        stats = sb("stats", [P, B, BLOCKS, 6])
        agg = sb("agg", [P, B, 2])
        dev = sb("dev", [P, B])
        spread = sb("spread", [P, B])
        scale1 = sb("scale1", [P, B])
        shift1 = sb("shift1", [P, B])
        acc_g = sb("acc_g", [P, P])
        acc_s = sb("acc_s", [P, 2 * P])
        ksum = sb("ksum", [P, 1])
        den_w = sb("den_w", [P, SUBS * DH])
        kv = sb("kv", [P, P])
        mix = sb("mix", [P, C])
        den = sb("den", [P, SUB])
        recip = sb("recip", [P, 2, SUB])
        stats2 = sb("stats2", [P, NCHUNK, 6])
        agg2 = sb("agg2", [P, 2])
        dev2 = sb("dev2", [P, 4])
        scale2 = sb("scale2", [P, 2])
        shift2 = sb("shift2", [P, 2])

        zeroed = sem("zeroed")
        wts_loaded = [sem(f"wts_loaded{k}") for k in range(4)]
        row0_loaded = sem("row0_loaded")
        raw_loaded = [sem(f"raw_loaded{s}") for s in range(RAW_SLOTS)]
        row_ready = [sem(f"row_ready{g}") for g in range(GROUPS)]
        high_ready = [sem(f"high_ready{g}") for g in range(GROUPS)]
        low_ready = [sem(f"low_ready{g}") for g in range(GROUPS)]
        down_ready = [sem(f"down_ready{g}") for g in range(GROUPS)]
        w_high_ready = [sem(f"w_high_ready{k}") for k in range(4)]
        w_low_ready = [sem(f"w_low_ready{k}") for k in range(4)]
        conv_done = [sem(f"conv_done{g}") for g in range(GROUPS)]
        saved = sem("saved")
        stored = sem("stored")
        consts_loaded, norm_loaded, proj_loaded = sem("consts_loaded"), sem("norm_loaded"), sem("proj_loaded")
        wt_done, wt_ready = sem("wt_done"), sem("wt_ready")
        stat_ready, stat_done = sem("stat_ready"), sem("stat_done")
        chain = sem("chain")
        yn_ready, tok_done, tok_ready = sem("yn_ready"), sem("tok_done"), sem("tok_ready")
        key_done, key_read, kp_ready, acc_used = sem("key_done"), sem("key_read"), sem("kp_ready"), sem("acc_used")
        query_done, query_read, qp_ready = sem("query_done"), sem("query_read"), sem("qp_ready")
        acc_read, small_done, small_read = sem("acc_read"), sem("small_done"), sem("small_read")
        recip_ready, normed, norm2 = sem("recip_ready"), sem("normed"), sem("norm2")
        bounced = sem("bounced")
        passed = sem("passed")
        var_ready, scale_ready = sem("var_ready"), sem("scale_ready")
        recip_sent = [sem(f"recip_sent{m}") for m in range(2)]
        proj_done, proj_read = sem("proj_done"), sem("proj_read")
        affine_ready, affine_done, fin_ready = sem("affine_ready"), sem("affine_done"), sem("fin_ready")

        def at_least(eng, s, n):
            if not isinstance(n, int) or n > 0:
                eng.wait_ge(s, n)

        def settled(eng):
            eng.sem_inc(passed, 1)

        def split_weights(eng, k):
            eng.wait_ge(wts_loaded[k], 64)
            eng.tensor_copy(w_high[:, k], wts[:, k]).then_inc(w_high_ready[k], 1)
            eng.wait_ge(w_high_ready[k], 1)
            eng.tensor_tensor(wts[:, k], wts[:, k], w_high[:, k], ALU.subtract).then_inc(w_high_ready[k], 1)
            eng.wait_ge(w_high_ready[k], 2)
            eng.tensor_scalar(w_low[:, k], wts[:, k], LOW_SCALE, None, ALU.mult).then_inc(w_low_ready[k], 1)

        def batches(eng, body):
            for b in (0, 1):
                body(b, b % 2, True, b >= 1, False)
            with eng.Fori(0, (B - 4) // 2) as n:
                for i in range(2):
                    body(n * 2 + (2 + i), i, True, True, True)
            for b in (B - 2, B - 1):
                body(b, b % 2, True, True, True)
            body(B, 0, False, True, True)
            body(B + 1, 1, False, False, True)

        def spread_heads(m, u):
            src = bounce[m, u * DH:u * DH + HEADS * SUBS, :]
            return bass.AP(tensor=src.tensor, offset=src.offset, ap=[[CHUNK, HEADS], [0, DH], [1, CHUNK]])

        bounce = nc.dram_tensor("bounce", (2, P, SUB), F32).ap()
        block = ctx.enter_context(nc.Block())

        @block.sync
        def _(sp):
            def load_weights(s, k):
                for pi, po, tap, pair in ((0, 0, 0, 0), (1, 1, 0, 0), (1, 0, 1, 0), (0, 1, 1, 1)):
                    n = TAPS - tap
                    sp.dma_start(wts[pi * C:(pi + 1) * C, s, pair:pair + n, po * C:(po + 1) * C],
                                 k[tap:KW:2, :, :].rearrange("t i o -> i t o")).then_inc(wts_loaded[s], 16)

            sp.dma_start(row0[0:C, :, 1:1 + W], x[:, :, 0, :].rearrange("b c w -> c b w")).then_inc(row0_loaded, 16)
            sp.dma_start(row0[C:P, :, 0:W], x[:, :, 0, :].rearrange("b c w -> c b w")).then_inc(row0_loaded, 16)
            sp.wait_ge(zeroed, 1)
            load_weights(0, k_td)
            for n in range(STEPS // RAW_ROWS):
                s = n % RAW_SLOTS
                h0 = 1 + n * RAW_ROWS
                if n >= RAW_SLOTS:
                    for g in range(GROUPS):
                        sp.wait_ge(row_ready[g], 1 + (n - RAW_SLOTS + 1) * RAW_ROWS)
                for half in range(2):
                    sp.dma_start(raw[half * C:(half + 1) * C, s, :, 1 - half:1 - half + RAW_ROWS * W],
                                 x[:, :, h0:h0 + RAW_ROWS, :].rearrange("b c h w -> c b (h w)"))\
                      .then_inc(raw_loaded[s], 16)
                if n == 1:
                    for s_, k in ((1, k_dt), (2, k_lr), (3, k_rl)):
                        load_weights(s_, k)
            sp.dma_start(cst[:, :], consts).then_inc(consts_loaded, 16)
            for d in range(2):
                sp.dma_start(wl[:, :, d, :], w_qkv.rearrange("(t o) c -> o t c", t=3)).then_inc(proj_loaded, 16)
            sp.dma_start(wol[:, :], w_out).then_inc(proj_loaded, 16)
            for n, v in enumerate((gn1_w, gn1_b, gn2_w, gn2_b)):
                for d in range(2):
                    sp.dma_start(norm[d * C:(d + 1) * C, n:n + 1], v.rearrange("(c a) -> c a", a=1))\
                      .then_inc(norm_loaded, 16)

            def tail(b, par, cur, prev, pp):
                if prev:
                    for m in range(2):
                        at_least(sp, recip_ready, 2 * (b - 1) + m + 1)
                        settled(sp)
                        at_least(sp, recip_sent[m], 64 * (b - 1))
                        settled(sp)
                        sp.dma_start(bounce[m], recip[:, m, :]).then_inc(bounced, 16)
                        at_least(sp, bounced, 16 * (2 * (b - 1) + m + 1))
                        settled(sp)
                        at_least(sp, normed, UNITS * (b - 1))
                        for u in range(4):
                            sp.dma_start(recip_b[:, 4 * m + u, :], spread_heads(m, u)).then_inc(recip_sent[m], 16)
                if pp:
                    at_least(sp, fin_ready, b - 1)
                    for d in range(2):
                        dst = out[bass.ds(b - 2, 1), :, :, :] if not isinstance(b, int) else out[b - 2:b - 1]
                        dst = dst.rearrange("o c (j d) w -> d (o c) j w", d=2)[d]
                        sp.dma_start(dst, fin[d * C:(d + 1) * C, :, :]).then_inc(stored, 16)

            batches(sp, tail)
            sp.wait_ge(stored, 32 * B)

        @block.gpsimd
        def _(pool):
            nc.gpsimd.memset(wts[:, :, TAPS - 1, 0:C], 0.0)
            nc.gpsimd.memset(wts[:, :, 0, C:P], 0.0).then_inc(zeroed, 1)
            nc.gpsimd.memset(high[:], 0.0)
            nc.gpsimd.memset(high_down[:], 0.0)
            nc.gpsimd.memset(low[:], 0.0).then_inc(zeroed, 1)
            nc.gpsimd.memset(w_q[:], 0.0)
            nc.gpsimd.memset(ones[:], 1.0)
            nc.gpsimd.memset(part[:], 1.0 / DH)
            nc.gpsimd.memset(half[:], -0.5)
            nc.gpsimd.memset(w_k[:], 0.0).then_inc(zeroed, 1)
            for k in range(1, 4):
                split_weights(pool, k)

            pool.wait_ge(var_ready, 1)
            nc.gpsimd.tensor_tensor(scale1[:, :], dev[:, :], half[:, :], ALU.pow).then_inc(scale_ready, 1)
            pool.wait_ge(scale_ready, 1)
            nc.gpsimd.tensor_scalar(scale1[:, :], scale1[:, :], norm[:, 0:1], None, ALU.mult).then_inc(scale_ready, 1)

            def tail(b, par, cur, prev, pp):
                if pp:
                    at_least(pool, small_read, 4 * (b - 1) + (3 if prev else 2))
                    nc.gpsimd.tensor_tensor(scale2[:, par:par + 1], dev2[:, 1:2], half[:, 0:1], ALU.pow)\
                        .then_inc(scale_ready, 1)
                    at_least(pool, scale_ready, 2 * b - 1)
                    settled(pool)
                    nc.gpsimd.tensor_scalar(scale2[:, par:par + 1], scale2[:, par:par + 1], norm[:, 2:3], None,
                                            ALU.mult).then_inc(scale_ready, 1)
                    at_least(pool, scale_ready, 2 * b)
                    settled(pool)
                    nc.gpsimd.tensor_scalar(shift2[:, par:par + 1], dev2[:, 3:4], scale2[:, par:par + 1],
                                            norm[:, 3:4], ALU.mult, ALU.add).then_inc(affine_ready, 1)
                if prev:
                    for u in range(UNITS):
                        if u % 4 == 0:
                            at_least(pool, recip_sent[u // 4], 64 * b)
                        nc.gpsimd.tensor_tensor(qp[:, 1 - par, u, :], qp[:, 1 - par, u, :], recip_b[:, u, :],
                                                ALU.mult).then_inc(normed, 1)
                if pp:
                    at_least(pool, affine_done, b - 1)
                    at_least(pool, stored, 32 * (b - 2))
                    nc.gpsimd.tensor_tensor(
                        fin[:, :, :].rearrange("p j w -> p w j"),
                        proj[:, par, :].rearrange("p (w j) -> p w j", j=J),
                        cols[:, :, bass.ds(b - 2, 1), :].rearrange("p w o j -> p w (o j)"), ALU.add)\
                        .then_inc(fin_ready, 1)

            batches(pool, tail)

        @block.tensor
        def _(pe):
            pe.wait_ge(zeroed, 2)
            for k in range(4):
                rows = (1, 64, 128, 191)[k]
                pe.wait_ge(w_low_ready[k], 1)
                with pe.Fori(0, STEPS - BODY + 1, BODY) as s:
                    for u in range(BODY):
                        for g in range(GROUPS):
                            pe.wait_ge(high_ready[g], s + (rows + u))
                            for part_n, (rows_16, ready, w) in enumerate(
                                    ((high, None, w_high), (high_down, down_ready, w_low), (low, low_ready, w_high))):
                                if ready is not None:
                                    pe.wait_ge(ready[g], s + (rows + u))
                                for d in range(TAPS):
                                    last = nc.tensor.matmul(conv[g][u % SLOTS][:, 0:GB * J], w[:, k, d, :],
                                                            rows_16[:, u % SLOTS, g * GB:(g + 1) * GB, d:d + J],
                                                            start=part_n == 0 and d == 0,
                                                            stop=part_n == 2 and d == TAPS - 1)
                            last.then_inc(conv_done[g], 1)

            pe.wait_ge(zeroed, 3)
            pe.wait_ge(consts_loaded, 16)
            pe.wait_ge(proj_loaded, 48)
            for n in range(3):
                nc.tensor.transpose(tok_ps[:, n * P:(n + 1) * P], wl[:, n].rearrange("p d c -> p (d c)"), ident)
            nc.tensor.transpose(acc_ps[:, 0:C], wol[:, :], cst[0:C, 0:C]).then_inc(wt_done, 1)
            for n, v in enumerate((agg[:, :, 0], spread[:, :])):
                pe.wait_ge(stat_ready, n + 1)
                nc.tensor.matmul(small_ps[:, n * B:(n + 1) * B], group_mean, v, start=True, stop=True)\
                    .then_inc(stat_done, 1)

            def keys(b, par, i):
                if isinstance(b, int) and b == 0 and i == 0:
                    pe.wait_ge(wt_ready, 1)
                at_least(pe, yn_ready, b + 1)
                at_least(pe, tok_ready, 4 * b + i)
                for n in range(4):
                    t = nc.tensor.transpose(tok_ps[:, n * P:(n + 1) * P], yn[:, par, (4 * i + n) * P:(4 * i + n + 1) * P],
                                            ident)
                t.then_inc(tok_done, 1)
                for m in (2 * i, 2 * i + 1):
                    at_least(pe, key_read, KBANKS * b + m - 1)
                    for n in range(2):
                        at = (2 * m + n) * P
                        k = nc.tensor.matmul(key_ps[m % 2][:, n * 2 * P:(n + 1) * 2 * P], yn[:, par, at:at + P],
                                             w_k[:, :, :].rearrange("p d n -> p (d n)"), start=True, stop=True)
                    k.then_inc(key_done, 1)

            def queries(b, par, i):
                for d in range(2):
                    u = 2 * i + d
                    at_least(pe, query_read, UNITS * b + u - 1)
                    nc.tensor.matmul(query_ps[d][:, :], w_q[:, d, :], yn[:, par, i * CHUNK:(i + 1) * CHUNK],
                                     start=True, stop=True).then_inc(query_done, 1)

            def gather(b, i):
                at_least(pe, kp_ready, KBANKS * b + 2 * i + 2)
                at_least(pe, tok_ready, 4 * b + i + 1)
                if i == 0:
                    at_least(pe, acc_read, b)
                for n in range(4):
                    for d in range(2):
                        nc.tensor.matmul(acc_ps[d * C:(d + 1) * C, 0:P], tok[:, i % 2, n * P + d * C:n * P + (d + 1) * C],
                                         kp[:, (2 * i + n // 2) % 4, (n % 2) * 2 * P + d * P:(n % 2) * 2 * P + (d + 1) * P],
                                         start=i == 0 and n == 0, stop=i == 3 and n == 3, skip_group_check=True)
                for n in range(4):
                    last = nc.tensor.matmul(acc_ps[DH * n:DH * (n + 1), P:3 * P], ones[:, :],
                                            kp[:, (2 * i + n // 2) % 4, (n % 2) * 2 * P:(n % 2 + 1) * 2 * P],
                                            start=False, stop=i == 3, skip_group_check=True)
                last.then_inc(acc_used, 1)

            def small(b, n, prev, pp):
                at_least(pe, small_read, 4 * (b - 1) + (n if prev else n // 2))
                if n == 0:
                    at_least(pe, proj_read, NCHUNK * (b - 1))
                    if prev:
                        at_least(pe, acc_read, b)
                        for d in range(2):
                            last = nc.tensor.matmul(small_ps[:, 0:1], acc_s[:, d * P:(d + 1) * P], part[:, :],
                                                    start=d == 0, stop=d == 1)
                        last = nc.tensor.matmul(small_ps[:, P:2 * P], w_v[:, :], acc_g[:, :], start=True, stop=True)
                    if pp:
                        at_least(pe, stat_ready, 2 * (b - 2) + 3)
                        last = nc.tensor.matmul(small_ps[:, 2 * P:2 * P + 1], group_mean, agg2[:, 0:1],
                                                start=True, stop=True)
                if n == 2:
                    if prev:
                        last = nc.tensor.matmul(small_ps[:, 0:C], kv[:, :], w_o[:, :], start=True, stop=True)
                    if pp:
                        at_least(pe, stat_ready, 2 * (b - 2) + 4)
                        last = nc.tensor.matmul(small_ps[:, 2 * P:2 * P + 1], group_mean, dev2[:, 2:3],
                                                start=True, stop=True)
                last.then_inc(small_done, 1)

            def denominators(b, par, m):
                at_least(pe, small_read, 4 * (b - 1) + 1 + 2 * m)
                at_least(pe, qp_ready, UNITS * (b - 1) + 4 * m + 4)
                for s in range(SUBS):
                    for u in range(4):
                        last = nc.tensor.matmul(small_ps[DH * u:DH * (u + 1), 0:SUB], den_w[:, s * DH:(s + 1) * DH],
                                                qp[:, 1 - par, 4 * m + u, s * SUB:(s + 1) * SUB],
                                                start=s == 0, stop=s == SUBS - 1)
                last.then_inc(small_done, 1)

            def outputs(b, par, chunks):
                for i in chunks:
                    at_least(pe, small_read, 4 * b)
                    at_least(pe, proj_read, NCHUNK * (b - 1) + i - 1)
                    at_least(pe, normed, UNITS * (b - 1) + 2 * i + 2)
                    for d in range(2):
                        last = nc.tensor.matmul(proj_ps[i % 2][d * C:(d + 1) * C, :], mix[:, :],
                                                qp[:, 1 - par, 2 * i + d, :], start=True, stop=True)
                    last.then_inc(proj_done, 1)

            def tail(b, par, cur, prev, pp):
                for i in range(4):
                    if i == 0 and prev:
                        gather(b - 1, 3)
                    if cur:
                        keys(b, par, i)
                    if i == 0 and (prev or pp):
                        small(b, 0, prev, pp)
                    if i == 1 and (prev or pp):
                        small(b, 2, prev, pp)
                    if cur:
                        queries(b, par, i)
                        if i > 0:
                            gather(b, i - 1)
                    if i in (0, 1) and prev:
                        denominators(b, par, i)
                    if i in (2, 3) and prev:
                        outputs(b, par, (2 * i - 4, 2 * i - 3))

            batches(pe, tail)

        @block.vector
        def _(dve):
            def low_part(slot, g, rows):
                gb = slice(g * GB, (g + 1) * GB)
                dve.wait_ge(row_ready[g], rows)
                nc.vector.tensor_tensor(low[:, slot, gb, HALO:HALO + J], state[:, slot, gb, :],
                                        high[:, slot, gb, HALO:HALO + J], ALU.subtract).then_inc(low_ready[g], 1)

            def start(g, rows, src):
                gb = slice(g * GB, (g + 1) * GB)
                nc.vector.tensor_copy(high[:, 0, gb, HALO:HALO + J], src).then_inc(high_ready[g], 1)
                nc.vector.tensor_copy(state[:, 0, gb, :], src).then_inc(row_ready[g], 1)
                low_part(0, g, rows)

            def step(u, g, rows, add):
                slot = (u + 1) % SLOTS
                gb = slice(g * GB, (g + 1) * GB)
                for to, ready in ((high[:, slot, gb, HALO:HALO + J], high_ready), (state[:, slot, gb, :], row_ready)):
                    nc.vector.scalar_tensor_tensor(
                        out=to, in0=conv[g][u % SLOTS][:, 0:GB * J].rearrange("p (b j) -> p b j", b=GB), scalar=0.0, in1=add,
                        op0=ALU.max, op1=ALU.add).then_inc(ready[g], 1)
                low_part(slot, g, rows)

            dve.wait_ge(row0_loaded, 32)
            dve.wait_ge(zeroed, 2)
            for g in range(GROUPS):
                start(g, 1, row0[:, g * GB:(g + 1) * GB, 1:1 + W:2])
            split_weights(dve, 0)

            for k in range(4):
                base = k * STEPS
                save = (1, 65, 128, 191)[k]
                rows = (1, 64, 128, 191)[k]
                if k == 2:
                    dve.wait_ge(saved, 128)
                    for g in range(GROUPS):
                        start(g, rows, cols[:, 0, g * GB:(g + 1) * GB, :])
                body = RAW_ROWS * RAW_SLOTS if k == 0 else BODY

                def steps(n, stat=None):
                    s = n * body
                    down = n * -body + (H - 2)
                    for u in range(body):
                        if k == 0 and u % RAW_ROWS == 0:
                            dve.wait_ge(raw_loaded[u // RAW_ROWS], n * 32 + 32)
                        dve.wait_ge(saved, s + max(save + u - 2, (1, 0, 0, 190)[k]))
                        for g in range(GROUPS):
                            gb = slice(g * GB, (g + 1) * GB)
                            if k == 0:
                                r = u % RAW_ROWS
                                add = raw[:, u // RAW_ROWS, gb, 1 + r * W:1 + (r + 1) * W:2]
                            elif k == 2:
                                add = cols[:, bass.ds(s + (u + 1), 1), gb, :].rearrange("p o b j -> p (o b) j")
                            else:
                                src = rows_h if k == 1 else cols
                                add = src[:, bass.ds(down - u, 1), gb, :].rearrange("p o b j -> p (o b) j")
                            dve.wait_ge(conv_done[g], s + (base + u + 1))
                            step(u, g, s + (rows + u + 1), add)
                        if stat is not None and u < B:
                            stat(u)

                if k < 3:
                    with dve.Fori(0, STEPS // body) as n:
                        steps(n)
                else:
                    steps(0)
                    with dve.Fori(1, BLOCKS) as n:
                        steps(n, lambda b: nc.vector.bn_stats(
                            stats[:, b, bass.ds(n - 1, 1), :].rearrange("p o s -> p (o s)"),
                            cols[:, bass.ds(W - n * BODY, BODY), b, :]))
            def link(ins, count):
                ins.then_inc(chain, 1)
                dve.wait_ge(chain, count)

            dve.wait_ge(saved, 254)
            dve.wait_ge(norm_loaded, 16 * 8)
            for b in range(B):
                last = nc.vector.bn_stats(stats[:, b, BLOCKS - 1, :], cols[:, 0:W - (BLOCKS - 1) * BODY, b, :])
            link(last, 1)
            for b in range(B):
                last = nc.vector.bn_aggr(agg[:, b, :], stats[:, b, :, :].rearrange("p n s -> p (n s)"))
            last.then_inc(stat_ready, 1)
            dve.wait_ge(stat_ready, 1)
            dve.wait_ge(stat_done, 1)
            mean1, var1 = small_ps[:, 0:B], small_ps[:, B:2 * B]
            link(nc.vector.scalar_tensor_tensor(out=dev[:, :], in0=mean1, scalar=-1.0, in1=agg[:, :, 0],
                                                op0=ALU.mult, op1=ALU.add), 2)
            link(nc.vector.tensor_tensor(dev[:, :], dev[:, :], dev[:, :], ALU.mult), 3)
            nc.vector.tensor_tensor(spread[:, :], dev[:, :], agg[:, :, 1], ALU.add).then_inc(stat_ready, 1)
            dve.wait_ge(stat_done, 2)
            nc.vector.tensor_scalar(dev[:, :], var1, EPS_GN, None, ALU.add).then_inc(var_ready, 1)
            dve.wait_ge(scale_ready, 2)
            link(nc.vector.scalar_tensor_tensor(out=shift1[:, :], in0=mean1, scalar=-1.0, in1=scale1[:, :],
                                                op0=ALU.mult, op1=ALU.mult), 4)
            link(nc.vector.tensor_scalar(shift1[:, :], shift1[:, :], norm[:, 1:2], None, ALU.add), 5)

            def normalise(b, par):
                at_least(dve, query_done, UNITS * (b - 1))
                one = lambda v: v[:, bass.ds(b, 1)]
                nc.vector.tensor_scalar(yn[:, par, :].rearrange("p (w j) -> p w j", j=J),
                                        cols[:, :, bass.ds(b, 1), :].rearrange("p w o j -> p w (o j)"),
                                        one(scale1), one(shift1), ALU.mult, ALU.add).then_inc(yn_ready, 1)

            def tokens(b, i):
                at_least(dve, tok_done, 4 * b + i + 1)
                at_least(dve, acc_used, 4 * b + i - 1)
                nc.vector.tensor_copy(tok[:, i % 2, :], tok_ps[:, :]).then_inc(tok_ready, 1)

            def elu1(out_, slot):
                return nc.vector.scalar_tensor_tensor(out=out_, in0=ex[:, slot, :], scalar=1.0, in1=re[:, slot, :],
                                                      op0=ALU.min, op1=ALU.add)

            def keys(b, i):
                for m in (2 * i, 2 * i + 1):
                    at_least(dve, key_read, KBANKS * b + m + 1)
                    at_least(dve, acc_used, 4 * b + m // 2 - 1)
                    elu1(kp[:, m % 4, :], m % 2).then_inc(kp_ready, 1)

            def queries(b, par, i):
                for u in (2 * i, 2 * i + 1):
                    at_least(dve, query_read, UNITS * b + u + 1)
                    at_least(dve, proj_done, NCHUNK * (b - 1))
                    elu1(qp[:, par, u, :], u % 2).then_inc(qp_ready, 1)

            def gathered(b):
                at_least(dve, acc_used, 4 * b)
                at_least(dve, small_read, 4 * (b - 1))
                nc.vector.tensor_copy(acc_g[:, :], acc_ps[:, 0:P])
                nc.vector.tensor_copy(acc_s[:, :], acc_ps[:, P:3 * P]).then_inc(acc_read, 1)

            def small(b, par, n, prev, pp):
                c = b - 2
                mean2 = small_ps[:, 2 * P:2 * P + 1]
                k = n if prev else n // 2
                at_least(dve, small_done, 4 * (b - 1) + k + 1)
                if n == 0:
                    if prev:
                        at_least(dve, small_read, 4 * (b - 1))
                        nc.vector.tensor_scalar(den_w[:, :], head_of, small_ps[:, 0:1], None, ALU.mult)
                        last = nc.vector.tensor_tensor(kv[:, :], small_ps[:, P:2 * P], same_head, ALU.mult)
                    if pp:
                        nc.vector.tensor_scalar(dev2[:, 3:4], mean2, -1.0, None, ALU.mult)
                        at_least(dve, stat_ready, 2 * c + 3)
                        last = nc.vector.scalar_tensor_tensor(out=dev2[:, 0:1], in0=mean2, scalar=-1.0,
                                                              in1=agg2[:, 0:1], op0=ALU.mult, op1=ALU.add)
                    last.then_inc(small_read, 1)
                    if pp:
                        at_least(dve, small_read, 4 * (b - 1) + 1)
                        nc.vector.tensor_scalar(dev2[:, 2:3], dev2[:, 0:1], dev2[:, 0:1], agg2[:, 1:2],
                                                ALU.mult, ALU.add).then_inc(stat_ready, 1)
                if n == 2:
                    if prev:
                        last = nc.vector.tensor_copy(mix[:, :], small_ps[:, 0:C])
                    if pp:
                        last = nc.vector.tensor_scalar(dev2[:, 1:2], mean2, EPS_GN, None, ALU.add)
                    last.then_inc(small_read, 1)
                if n % 2:
                    m = n // 2
                    at_least(dve, recip_ready, 2 * (b - 1) + m)
                    nc.vector.tensor_scalar(den[:, :], small_ps[:, 0:SUB], EPS_ATTN, None, ALU.add).then_inc(small_read, 1)
                    at_least(dve, small_read, 4 * (b - 1) + n + 1)
                    at_least(dve, bounced, 16 * (2 * (b - 2) + m + 1))
                    nc.vector.reciprocal(recip[:, m, :], den[:, :]).then_inc(recip_ready, 1)

            def tail(b, par, cur, prev, pp):
                if pp:
                    at_least(dve, proj_read, NCHUNK * (b - 1))
                    for i in range(NCHUNK):
                        last = nc.vector.bn_stats(stats2[:, i, :], proj[:, par, i * CHUNK:(i + 1) * CHUNK])
                    last.then_inc(norm2, 1)
                    at_least(dve, norm2, b - 1)
                    settled(dve)
                    nc.vector.bn_aggr(agg2[:, :], stats2[:, :, :].rearrange("p n s -> p (n s)")).then_inc(stat_ready, 1)
                for i in range(4):
                    if i == 0 and prev:
                        gathered(b)
                    if cur:
                        tokens(b, i)
                    if i in (1, 2) and prev:
                        small(b, par, 2 * i - 1, prev, pp)
                    if cur:
                        keys(b, i)
                    if i == 0 and (prev or pp):
                        small(b, par, 0, prev, pp)
                    if i == 1 and (prev or pp):
                        small(b, par, 2, prev, pp)
                    if cur:
                        queries(b, par, i)
                    if i == 2 and cur and not (isinstance(b, int) and b == B - 1):
                        normalise(b + 1, 1 - par)

            normalise(0, 0)
            batches(dve, tail)

        @block.scalar
        def _(act):
            def down(slot, n):
                for g in range(GROUPS):
                    gb = slice(g * GB, (g + 1) * GB)
                    act.wait_ge(high_ready[g], n)
                    act.activation(high_down[:, slot, gb, HALO:HALO + J], high[:, slot, gb, HALO:HALO + J], ACT.Copy,
                                   scale=1.0 / LOW_SCALE).then_inc(down_ready[g], 1)
                for g in range(GROUPS):
                    act.wait_ge(row_ready[g], n)

            def save(slot, to):
                act.activation(to, state[:, slot, :, :], ACT.Copy).then_inc(saved, 1)

            def scatter(slot, ph, jh, s=None):
                for pw in range(2):
                    dst = cols_w[ph * C:(ph + 1) * C, :].rearrange("p (w two b j) -> p w two b j", two=2, b=B, j=J)
                    dst = dst[:, :, pw, :, bass.ds(jh, 1)].rearrange("p w b o -> p (o b) w")
                    last = act.activation(dst, state[pw * C:(pw + 1) * C, slot, :, :], ACT.Copy)
                last.then_inc(saved, 1)

            down(0, 1)
            save(0, rows_h[:, 0])
            with act.Fori(0, STEPS - BODY + 1, BODY) as s:
                for u in range(BODY):
                    down((u + 1) % SLOTS, s + (u + 2))
                    save((u + 1) % SLOTS, rows_h[:, bass.ds(s + (u + 1), 1), :, :].rearrange("p o b j -> p (o b) j"))
            scatter(0, 1, J - 1)
            with act.Fori(0, STEPS // 6) as n:
                for u in range(6):
                    down((u + 1) % SLOTS, n * 6 + (65 + u))
                    scatter((u + 1) % SLOTS, u % 2, n * -3 + (H // 2 - 1 - (u + 1) // 2))
            for s in range(STEPS - STEPS % 6, STEPS):
                h = H - 2 - s
                down((s + 1) % SLOTS, 65 + s)
                scatter((s + 1) % SLOTS, h % 2, h // 2)
            down(0, 128)
            for k, rows in ((2, 129), (3, 192)):
                with act.Fori(0, STEPS // BODY) as n:
                    for u in range(BODY):
                        down((u + 1) % SLOTS, n * BODY + (rows + u))
                        w = n * BODY + (u + 1) if k == 2 else n * -BODY + (W - 2 - u)
                        save((u + 1) % SLOTS, cols[:, bass.ds(w, 1), :, :].rearrange("p o b j -> p (o b) j"))

            act.wait_ge(wt_done, 1)
            for n, w in ((0, w_q), (1, w_k)):
                for d in range(2):
                    act.activation(w[d * C:(d + 1) * C, d, :], tok_ps[d * C:(d + 1) * C, n * P:(n + 1) * P], ACT.Copy)
            act.activation(w_v[:, :], tok_ps[:, 2 * P:3 * P], ACT.Copy)
            act.activation(w_o[:, :], acc_ps[:, 0:C], ACT.Copy).then_inc(wt_ready, 1)

            def elu_parts(ps, slot, read):
                act.activation(ex[:, slot, :], ps, ACT.Exp)
                act.activation(re[:, slot, :], ps, ACT.Relu).then_inc(read, 1)

            def collect(b, par, chunks):
                for i in chunks:
                    at_least(act, proj_done, NCHUNK * (b - 1) + i + 1)
                    at_least(act, fin_ready, b - 2)
                    act.activation(proj[:, 1 - par, i * CHUNK:(i + 1) * CHUNK], proj_ps[i % 2][:, :], ACT.Copy)\
                       .then_inc(proj_read, 1)

            def tail(b, par, cur, prev, pp):
                for i in range(4):
                    if cur:
                        for m in (2 * i, 2 * i + 1):
                            at_least(act, key_done, KBANKS * b + m + 1)
                            at_least(act, qp_ready, UNITS * b + m - 1)
                            elu_parts(key_ps[m % 2][:, :], m % 2, key_read)
                    if i == 2 and pp:
                        at_least(act, affine_ready, b - 1)
                        act.activation(proj[:, par, :], proj[:, par, :], ACT.Identity, bias=shift2[:, par:par + 1],
                                       scale=scale2[:, par:par + 1]).then_inc(affine_done, 1)
                    if cur:
                        for u in (2 * i, 2 * i + 1):
                            at_least(act, query_done, UNITS * b + u + 1)
                            at_least(act, kp_ready, KBANKS * b + u + 1)
                            elu_parts(query_ps[u % 2][:, :], u % 2, query_read)
                    if i in (2, 3) and prev:
                        collect(b, par, (2 * i - 4, 2 * i - 3))

            batches(act, tail)


_INS = ["x", "L0_conv_k_td", "L0_conv_k_dt", "L0_conv_k_lr", "L0_conv_k_rl", "L1_conv_gn1_w", "L1_conv_gn1_b",
        "L1_conv_w_qkv", "L1_conv_w_out", "L1_conv_gn2_w", "L1_conv_gn2_b"]


def kernel(**inputs):
    import concourse.bacc as bacc
    from concourse.bass_utils import run_bass_kernel_spmd

    nc = bacc.Bacc("TRN2", target_bir_lowering=False, num_devices=1)
    arrays = {name: np.ascontiguousarray(inputs[name]) for name in _INS}
    arrays["consts"] = constants()
    args = [nc.dram_tensor(name, a.shape, mybir.dt.from_np(a.dtype), kind="ExternalInput").ap()
            for name, a in arrays.items()]
    args.append(nc.dram_tensor("out", (B, C, H, W), F32, kind="ExternalOutput").ap())
    build(nc, *args)
    r = run_bass_kernel_spmd(nc, [arrays], core_ids=[0])
    return r.results[0]["out"]
```

```python
import numpy as np

import concourse.bass as bass
from concourse import mybir
from contextlib import ExitStack

F32 = mybir.dt.float32
F16 = mybir.dt.float16
ALU = mybir.AluOpType
ACT = mybir.ActivationFunctionType

B, C, H, W = 8, 64, 64, 64
KW = 9
P = 2 * C
J = W // 2
HALO = 2
RJ = J + 2 * HALO
TAPS = 2 * HALO + 1
ROW = B * J
STEPS = H - 1
GROUPS = 2
GB = B // GROUPS
SLOTS = 3
LOW_SCALE = 256.0
PROJ_SCALE = 2.0
BODY = 9
LONG_BODY = 21
RAW_ROWS = 7
RAW_SLOTS = 3
RAW_B = RAW_ROWS * W + 2
assert H == W and STEPS % BODY == 0 and LONG_BODY == RAW_ROWS * RAW_SLOTS and STEPS % LONG_BODY == 0


HEADS, DH = 4, 32
assert HEADS * DH == P
NW = W * J
CHUNK = 512
NCHUNK = NW // CHUNK
UNITS = 2 * NCHUNK
KBANKS = NW // 2 // P
EPS_GN, EPS_ATTN = 1e-5, 1e-6
SUBS = 4
SUB = CHUNK // SUBS
HALVES = slice(0, J // 2), slice(J // 2, J)
BLOCKS = STEPS // BODY


def constants():
    p = np.arange(P)
    head = p // DH
    group = (p % C) // 2
    row = np.arange(SUBS * DH)
    places = SUBS * head[:, None] + (row // DH)[None, :] == (row % DH)[None, :]
    return np.concatenate([np.eye(P), head[:, None] == head[None, :], (group[:, None] == group[None, :]) / 4.0,
                           places], axis=1).astype(np.float32)


def build(nc, x, k_td, k_dt, k_lr, k_rl, gn1_w, gn1_b, w_qkv, w_out, gn2_w, gn2_b, consts, out):
    with ExitStack() as ctx:
        def sb(name, shape, dt=F32):
            return ctx.enter_context(nc.sbuf_tensor(name, shape, dt))

        def sem(name):
            return ctx.enter_context(nc.semaphore(name))

        scan_rows = sb("scan_rows", [P, SLOTS * ROW + B * (W + 2)])
        state = scan_rows[:, 0:SLOTS * ROW].rearrange("p (s b j) -> p s b j", s=SLOTS, b=B)
        parts = sb("parts", [P, 4 * NW], F16)
        nw, nr = 4 * TAPS * P, SLOTS * B * RJ
        w_high, w_low = (parts[:, n * nw:(n + 1) * nw].rearrange("p (s t n) -> p s t n", s=4, t=TAPS) for n in range(2))
        high, low, high_down = (parts[:, 2 * nw + n * nr:2 * nw + (n + 1) * nr]
                                .rearrange("p (s b j) -> p s b j", s=SLOTS, b=B) for n in range(3))
        stacked = parts[:, :].rearrange("p (r d n) -> p r d n", r=2, d=2)
        rows_h = sb("rows_h", [P, H, B, J])
        cols_w = sb("cols_w", [P, W * B * J])
        bank = [ctx.enter_context(nc.psum_tensor(f"bank{n}", [P, 512], F32)) for n in range(8)]
        conv = ((bank[0], bank[4], bank[6]), (bank[1], bank[5], bank[7]))
        key_ps, tok_ps, acc_ps, query_ps, small_ps, out_ps = bank[0:2], bank[2], bank[3], bank[4:6], bank[6], bank[7]
        proj_ps = (out_ps, small_ps, out_ps, out_ps)
        cols = cols_w[:, :].rearrange("p (w b j) -> p w b j", w=W, b=B)
        raw = cols_w[:, 0:RAW_SLOTS * B * RAW_B].rearrange("p (s b e) -> p s b e", s=RAW_SLOTS, b=B)
        row0 = scan_rows[:, SLOTS * ROW:].rearrange("p (b w) -> p b w", b=B)
        flat_h = rows_h[:, :, :, :].rearrange("p h b j -> p (h b j)")
        qp = flat_h[:, 0:2 * UNITS * CHUNK].rearrange("p (r u n) -> p r u n", r=2, u=UNITS)
        recip_b = flat_h[:, 2 * UNITS * CHUNK:3 * UNITS * CHUNK].rearrange("p (u n) -> p u n", u=UNITS)
        proj = flat_h[:, 3 * UNITS * CHUNK:3 * UNITS * CHUNK + 2 * NW].rearrange("p (r n) -> p r n", r=2)
        yn = sb("yn", [P, 2, NW])
        wts = yn[:, :, :].rearrange("p r n -> p (r n)")[:, 0:4 * TAPS * P].rearrange("p (s t n) -> p s t n", s=4, t=TAPS)
        tok = sb("tok", [P, 2, 512])
        kp = sb("kp", [P, 4, 512])
        ex = sb("ex", [P, 4, 512])
        re = scan_rows[:, 0:1024].rearrange("p (s n) -> p s n", s=2)
        fin = sb("fin", [P, J, W])
        fin_last = flat_h[:, 2 * UNITS * CHUNK:2 * UNITS * CHUNK + J * W].rearrange("p (j w) -> p j w", j=J)
        cst = sb("cst", [P, 3 * P + SUBS * DH])
        ident, same_head, group_mean, head_of = (cst[:, 0:P], cst[:, P:2 * P], cst[:, 2 * P:3 * P],
                                                 cst[:, 3 * P:3 * P + SUBS * DH])
        ones = sb("ones", [P, DH])
        row_of_ones = sb("row_of_ones", [1, 512], F16)
        minus_one = sb("minus_one", [P, 1])
        part = sb("part", [P, 1])
        half = sb("half", [P, B])
        wl = sb("wl", [P, 3, 2, C])
        wol = sb("wol", [C, P])
        w_two = sb("w_two", [P, 2, P])
        w_two_high = sb("w_two_high", [P, 2, P], F16)
        w_two_low = sb("w_two_low", [P, 2, 2, P], F16)
        two_idents = sb("two_idents", [P, C], F16)
        w_v = sb("w_v", [P, P])
        w_o = sb("w_o", [P, C])
        norm = sb("norm", [P, 4])
        stats = tok[:, :, :].rearrange("p r n -> p (r n)")[:, 0:B * (2 * BLOCKS - 1) * 6]\
            .rearrange("p (b s k) -> p b s k", b=B, s=2 * BLOCKS - 1)
        agg = sb("agg", [P, B, 2])
        dev = sb("dev", [P, B])
        spread = sb("spread", [P, B])
        scale1 = sb("scale1", [P, B])
        bias1 = sb("bias1", [P, 1])
        shift1 = sb("shift1", [P, B])
        acc_g = sb("acc_g", [P, P])
        acc_s = sb("acc_s", [P, 2 * P])
        den_w = sb("den_w", [P, SUBS * DH])
        kv = sb("kv", [P, P])
        mix = sb("mix", [P, C])
        den = sb("den", [P, SUB])
        recip = sb("recip", [P, 2, SUB])
        stats2 = sb("stats2", [P, NCHUNK, 6])
        agg2 = sb("agg2", [P, 2])
        dev2 = sb("dev2", [P, 4])
        scale2 = sb("scale2", [P, 2])
        shift2 = sb("shift2", [P, 2])

        zeroed = sem("zeroed")
        wts_loaded = [sem(f"wts_loaded{k}") for k in range(4)]
        row0_loaded = sem("row0_loaded")
        raw_loaded = [sem(f"raw_loaded{s}") for s in range(RAW_SLOTS)]
        row_ready = [sem(f"row_ready{g}") for g in range(GROUPS)]
        high_ready = [sem(f"high_ready{g}") for g in range(GROUPS)]
        low_ready = [sem(f"low_ready{g}") for g in range(GROUPS)]
        down_ready = [sem(f"down_ready{g}") for g in range(GROUPS)]
        w_high_ready = [sem(f"w_high_ready{k}") for k in range(4)]
        w_low_ready = [sem(f"w_low_ready{k}") for k in range(4)]
        conv_done = [sem(f"conv_done{g}") for g in range(GROUPS)]
        saved = sem("saved")
        stored = sem("stored")
        consts_loaded, norm_loaded, proj_loaded = sem("consts_loaded"), sem("norm_loaded"), sem("proj_loaded")
        wt_done, wt_ready = sem("wt_done"), sem("wt_ready")
        stat_ready, stat_done = sem("stat_ready"), sem("stat_done")
        chain = sem("chain")
        high_part, low_part = sem("high_part"), sem("low_part")
        first_yn, first_high, first_low = sem("first_yn"), sem("first_high"), sem("first_low")
        yn_ready, tok_done, tok_ready = sem("yn_ready"), sem("tok_done"), sem("tok_ready")
        key_done, key_exp, kp_ready, acc_used = sem("key_done"), sem("key_exp"), sem("kp_ready"), sem("acc_used")
        query_done, query_read, qp_ready = sem("query_done"), sem("query_read"), sem("qp_ready")
        acc_read, small_done, small_read = sem("acc_read"), sem("small_done"), sem("small_read")
        recip_ready, normed, norm2 = sem("recip_ready"), sem("normed"), sem("norm2")
        bounced = sem("bounced")
        passed = sem("passed")
        var_ready, scale_ready = sem("var_ready"), sem("scale_ready")
        recip_sent = [sem(f"recip_sent{m}") for m in range(2)]
        normed_last = sem("normed_last")
        proj_done, proj_read = sem("proj_done"), sem("proj_read")
        affine_ready, affine_done, fin_ready = sem("affine_ready"), sem("affine_done"), sem("fin_ready")

        def at_least(eng, s, n):
            if not isinstance(n, int) or n > 0:
                eng.wait_ge(s, n)

        def settled(eng):
            eng.sem_inc(passed, 1)

        def split_weights(eng, k):
            eng.wait_ge(wts_loaded[k], 64)
            eng.tensor_copy(w_high[:, k], wts[:, k]).then_inc(w_high_ready[k], 1)
            eng.wait_ge(w_high_ready[k], 1)
            eng.tensor_tensor(wts[:, k], wts[:, k], w_high[:, k], ALU.subtract).then_inc(w_high_ready[k], 1)
            eng.wait_ge(w_high_ready[k], 2)
            eng.tensor_scalar(w_low[:, k], wts[:, k], LOW_SCALE, None, ALU.mult).then_inc(w_low_ready[k], 1)

        def small_step(b, n):
            if isinstance(b, int):
                return n + 1 if b == 1 else 6 * b - 8 + (n - 3 if b == B + 1 else n + 1)
            return b * 6 + (n - 7)

        def chunk_of(i):
            return slice(i * CHUNK, (i + 1) * CHUNK)

        def has_next(b, cur):
            return cur and not (isinstance(b, int) and b == B - 1)

        def low_of(eng, b, par, d, ready):
            at_least(eng, high_part, 2 * b + (d + 1))
            here, there = slice(d * C, (d + 1) * C), slice((1 - d) * C, (2 - d) * C)
            eng.tensor_tensor(stacked[there, par, d], yn[here, par], stacked[here, par, d], ALU.subtract)\
               .then_inc(ready, 1)

        def batches(eng, body):
            for b in (0, 1):
                body(b, b % 2, True, b >= 1, False)
            with eng.Fori(0, (B - 4) // 2) as n:
                for i in range(2):
                    body(n * 2 + (2 + i), i, True, True, True)
            for b in (B - 2, B - 1):
                body(b, b % 2, True, True, True)
            body(B, 0, False, True, True)
            body(B + 1, 1, False, False, True)

        def spread_heads(m, u):
            src = bounce[m, u * DH:u * DH + HEADS * SUBS, :]
            return bass.AP(tensor=src.tensor, offset=src.offset, ap=[[CHUNK, HEADS], [0, DH], [1, CHUNK]])

        bounce = nc.dram_tensor("bounce", (2, P, SUB), F32).ap()
        block = ctx.enter_context(nc.Block())

        @block.sync
        def _(sp):
            def load_weights(s, k):
                for pi, po, tap, pair in ((0, 0, 0, 0), (1, 1, 0, 0), (1, 0, 1, 0), (0, 1, 1, 1)):
                    n = TAPS - tap
                    sp.dma_start(wts[pi * C:(pi + 1) * C, s, pair:pair + n, po * C:(po + 1) * C],
                                 k[tap:KW:2, :, :].rearrange("t i o -> i t o")).then_inc(wts_loaded[s], 16)

            sp.dma_start(row0[0:C, :, 1:1 + W], x[:, :, 0, :].rearrange("b c w -> c b w")).then_inc(row0_loaded, 16)
            sp.dma_start(row0[C:P, :, 0:W], x[:, :, 0, :].rearrange("b c w -> c b w")).then_inc(row0_loaded, 16)
            sp.wait_ge(zeroed, 1)
            load_weights(0, k_td)
            for n in range(STEPS // RAW_ROWS):
                s = n % RAW_SLOTS
                h0 = 1 + n * RAW_ROWS
                if n >= RAW_SLOTS:
                    for g in range(GROUPS):
                        sp.wait_ge(row_ready[g], 1 + (n - RAW_SLOTS + 1) * RAW_ROWS)
                for half in range(2):
                    sp.dma_start(raw[half * C:(half + 1) * C, s, :, 1 - half:1 - half + RAW_ROWS * W],
                                 x[:, :, h0:h0 + RAW_ROWS, :].rearrange("b c h w -> c b (h w)"))\
                      .then_inc(raw_loaded[s], 16)
                if n == 1:
                    for s_, k in ((1, k_dt), (2, k_lr), (3, k_rl)):
                        load_weights(s_, k)
            sp.dma_start(cst[:, :], consts).then_inc(consts_loaded, 16)
            for d in range(2):
                sp.dma_start(wl[:, :, d, :], w_qkv.rearrange("(t o) c -> o t c", t=3)).then_inc(proj_loaded, 16)
            sp.dma_start(wol[:, :], w_out).then_inc(proj_loaded, 16)
            for n, v in enumerate((gn1_w, gn1_b, gn2_w, gn2_b)):
                for d in range(2):
                    sp.dma_start(norm[d * C:(d + 1) * C, n:n + 1], v.rearrange("(c a) -> c a", a=1))\
                      .then_inc(norm_loaded, 16)

            def broadcast(c, m):
                at_least(sp, recip_ready, 2 * c + m + 1)
                settled(sp)
                at_least(sp, recip_sent[m], 64 * c)
                settled(sp)
                sp.dma_start(bounce[m], recip[:, m, :]).then_inc(bounced, 16)
                at_least(sp, bounced, 16 * (2 * c + m + 1))
                settled(sp)
                at_least(sp, normed, UNITS * c)
                for u in range(4):
                    sp.dma_start(recip_b[:, 4 * m + u, :], spread_heads(m, u)).then_inc(recip_sent[m], 16)

            def store(c, rows, fin=fin):
                for d in range(2):
                    dst = out[bass.ds(c, 1), :, :, :] if not isinstance(c, int) else out[c:c + 1]
                    dst = dst.rearrange("o c (j d) w -> d (o c) j w", d=2)[d]
                    sp.dma_start(dst[:, rows, :], fin[d * C:(d + 1) * C, rows, :]).then_inc(stored, 16)

            for c in range(2):
                for m in range(2):
                    broadcast(c, m)
            with sp.Fori(0, (B - 4) // 2) as n:
                for i in range(2):
                    c = n * 2 + (2 + i)
                    for m in range(2):
                        broadcast(c, m)
                    at_least(sp, fin_ready, n * 2 + (i + 2))
                    settled(sp)
                    store(n * 2 + i, slice(0, J))
            for m in range(2):
                broadcast(B - 2, m)
            sp.wait_ge(fin_ready, B - 2)
            store(B - 4, slice(0, J))
            for m in range(2):
                broadcast(B - 1, m)
            for c in (B - 3, B - 2):
                sp.wait_ge(fin_ready, c + 2)
                store(c, slice(0, J))
            for h, rows in enumerate(HALVES):
                sp.wait_ge(fin_ready, B + 1 + h)
                store(B - 1, rows, fin_last)
            sp.wait_ge(stored, 1 + 32 * (B + 1))

        @block.gpsimd
        def _(pool):
            nc.gpsimd.memset(wts[:, :, TAPS - 1, 0:C], 0.0)
            nc.gpsimd.memset(wts[:, :, 0, C:P], 0.0).then_inc(zeroed, 1)
            nc.gpsimd.memset(high[:, :, :, :], 0.0)
            nc.gpsimd.memset(high_down[:, :, :, :], 0.0)
            nc.gpsimd.memset(low[:, :, :, :], 0.0).then_inc(zeroed, 1)
            for count in (affine_ready, fin_ready, stored):
                pool.sem_inc(count, 1)
            nc.gpsimd.memset(ones[:], 1.0)
            nc.gpsimd.memset(row_of_ones[:], 1.0)
            nc.gpsimd.memset(minus_one[:], -1.0)
            nc.gpsimd.memset(part[:], 1.0 / DH)
            nc.gpsimd.memset(half[:], -0.5)
            nc.gpsimd.memset(w_two_low[:], 0.0).then_inc(zeroed, 1)
            for k in range(1, 4):
                split_weights(pool, k)

            pool.wait_ge(var_ready, 1)
            nc.gpsimd.tensor_tensor(scale1[:, :], dev[:, :], half[:, :], ALU.pow).then_inc(scale_ready, 1)
            pool.wait_ge(scale_ready, 1)
            nc.gpsimd.tensor_scalar(scale1[:, :], scale1[:, :], norm[:, 0:1], 1.0 / PROJ_SCALE, ALU.mult,
                                    ALU.mult).then_inc(scale_ready, 1)

            def normalise_units(b, par, m):
                at_least(pool, recip_sent[m], 64 * b)
                for u in range(4 * m, 4 * m + 4):
                    nc.gpsimd.tensor_tensor(qp[:, 1 - par, u, :], qp[:, 1 - par, u, :], recip_b[:, u, :],
                                            ALU.mult).then_inc(normed, 1)

            def iteration(b, par, cur, prev, pp):
                if cur and prev:
                    normalise_units(b, par, 0)
                if pp:
                    at_least(pool, small_read, small_step(b, 5))
                    nc.gpsimd.tensor_tensor(scale2[:, par:par + 1], dev2[:, 1:2], half[:, 0:1], ALU.pow)\
                        .then_inc(scale_ready, 1)
                    at_least(pool, scale_ready, 2 * b - 1)
                    settled(pool)
                    nc.gpsimd.tensor_scalar(scale2[:, par:par + 1], scale2[:, par:par + 1], norm[:, 2:3], None,
                                            ALU.mult).then_inc(scale_ready, 1)
                    at_least(pool, scale_ready, 2 * b)
                    settled(pool)
                    nc.gpsimd.tensor_scalar(shift2[:, par:par + 1], dev2[:, 3:4], scale2[:, par:par + 1],
                                            norm[:, 3:4], ALU.mult, ALU.add).then_inc(affine_ready, 1)
                if cur and prev:
                    normalise_units(b, par, 1)
                if pp and prev:
                    at_least(pool, affine_done, b - 1)
                    at_least(pool, stored, b * 32 - 63)
                    nc.gpsimd.tensor_tensor(
                        fin[:, :, :].rearrange("p j w -> p w j"),
                        proj[:, par, :].rearrange("p (w j) -> p w j", j=J),
                        cols[:, :, bass.ds(b - 2, 1), :].rearrange("p w o j -> p w (o j)"), ALU.add)\
                        .then_inc(fin_ready, 1)

            batches(pool, iteration)

        @block.tensor
        def _(pe):
            pe.wait_ge(zeroed, 2)
            for k in range(4):
                rows = (1, 64, 128, 191)[k]
                pe.wait_ge(w_low_ready[k], 1)
                with pe.Fori(0, STEPS - BODY + 1, BODY) as s:
                    for u in range(BODY):
                        for g in range(GROUPS):
                            pe.wait_ge(high_ready[g], s + (rows + u))
                            for part_n, (rows_16, ready, w) in enumerate(
                                    ((high, None, w_high), (high_down, down_ready, w_low), (low, low_ready, w_high))):
                                if ready is not None:
                                    pe.wait_ge(ready[g], s + (rows + u))
                                for d in range(TAPS):
                                    last = nc.tensor.matmul(conv[g][u % SLOTS][:, 0:GB * J], w[:, k, d, :],
                                                            rows_16[:, u % SLOTS, g * GB:(g + 1) * GB, d:d + J],
                                                            start=part_n == 0 and d == 0,
                                                            stop=part_n == 2 and d == TAPS - 1)
                            last.then_inc(conv_done[g], 1)

            pe.wait_ge(zeroed, 3)
            pe.wait_ge(consts_loaded, 16)
            pe.wait_ge(proj_loaded, 48)
            for n in range(3):
                nc.tensor.transpose(tok_ps[:, n * P:(n + 1) * P], wl[:, n].rearrange("p d c -> p (d c)"), ident)
            nc.tensor.transpose(acc_ps[:, 0:C], wol[:, :], cst[0:C, 0:C]).then_inc(wt_done, 1)
            for n, v in enumerate((agg[:, :, 0], spread[:, :])):
                pe.wait_ge(stat_ready, n + 1)
                nc.tensor.matmul(small_ps[:, n * B:(n + 1) * B], group_mean, v, start=True, stop=True)\
                    .then_inc(stat_done, 1)

            def token_major(b, par, i):
                first = isinstance(b, int) and b == 0
                if first and i == 0:
                    pe.wait_ge(wt_ready, 2)
                if first and i < NCHUNK - 1:
                    pe.wait_ge(first_low, 2 * i + 2)
                elif first or i == 0:
                    at_least(pe, low_part, 2 * (b + 1))
                at_least(pe, tok_ready, 4 * b + i)
                for n in range(4):
                    at = (4 * i + n) * P
                    for d in range(2):
                        t = nc.tensor.matmul(tok_ps[:, n * P + d * C:n * P + (d + 1) * C],
                                             stacked[:, par, d, at:at + P], two_idents[:, :], start=True, stop=True)
                t.then_inc(tok_done, 1)

            def keys(b, par, i):
                for m in (2 * i, 2 * i + 1):
                    at_least(pe, kp_ready, KBANKS * b + m - 1)
                    nc.tensor.matmul(key_ps[m % 2][:, :], row_of_ones[:, 0:P], row_of_ones[:, :], start=True, stop=False)
                    for n in range(2):
                        at = (2 * m + n) * P
                        for d in range(2):
                            for part_n, w in enumerate((w_two_high[:, 1], w_two_low[:, d, 1])):
                                k = nc.tensor.matmul(key_ps[m % 2][:, (2 * n + d) * P:(2 * n + d + 1) * P],
                                                     stacked[:, par, d, at:at + P], w,
                                                     start=False, stop=n == d == part_n == 1)
                    k.then_inc(key_done, 1)

            def queries(b, par, i):
                for d in range(2):
                    u = 2 * i + d
                    at_least(pe, query_read, UNITS * b + u - 1)
                    for part_n, w in enumerate((w_two_high[:, 0], w_two_low[:, d, 0])):
                        q = nc.tensor.matmul(query_ps[d][:, :], w, stacked[:, par, d, i * CHUNK:(i + 1) * CHUNK],
                                             start=part_n == 0, stop=part_n == 1)
                    q.then_inc(query_done, 1)

            def gather(b, i):
                at_least(pe, kp_ready, KBANKS * b + 2 * i + 2)
                at_least(pe, tok_ready, 4 * b + i + 1)
                if i == 0:
                    at_least(pe, acc_read, b)
                for n in range(4):
                    for d in range(2):
                        nc.tensor.matmul(acc_ps[d * C:(d + 1) * C, 0:P], tok[:, i % 2, n * P + d * C:n * P + (d + 1) * C],
                                         kp[:, (2 * i + n // 2) % 4, (n % 2) * 2 * P + d * P:(n % 2) * 2 * P + (d + 1) * P],
                                         start=i == 0 and n == 0, stop=i == 3 and n == 3, skip_group_check=True)
                for n in range(4):
                    last = nc.tensor.matmul(acc_ps[DH * n:DH * (n + 1), P:3 * P], ones[:, :],
                                            kp[:, (2 * i + n // 2) % 4, (n % 2) * 2 * P:(n % 2 + 1) * 2 * P],
                                            start=False, stop=i == 3, skip_group_check=True)
                last.then_inc(acc_used, 1)

            def small(b, n, prev):
                at_least(pe, small_read, small_step(b, n) - 1)
                if n == 0 or not prev and n == 4:
                    at_least(pe, proj_read, NCHUNK * (b - 2) + 2)
                if n == 0:
                    at_least(pe, acc_read, b)
                    for d in range(2):
                        nc.tensor.matmul(small_ps[:, 0:1], acc_s[:, d * P:(d + 1) * P], part[:, :],
                                         start=d == 0, stop=d == 1)
                    last = nc.tensor.matmul(small_ps[:, P:2 * P], w_v[:, :], acc_g[:, :], start=True, stop=True)
                if n == 2:
                    last = nc.tensor.matmul(small_ps[:, 0:C], kv[:, :], w_o[:, :], start=True, stop=True)
                if n >= 4:
                    at_least(pe, stat_ready, 2 * (b - 2) + n - 1)
                    last = nc.tensor.matmul(small_ps[:, 0:1], group_mean, agg2[:, 0:1] if n == 4 else dev2[:, 2:3],
                                            start=True, stop=True)
                last.then_inc(small_done, 1)

            def denominators(b, par, m):
                at_least(pe, small_read, small_step(b, 2 * m + 1) - 1)
                at_least(pe, qp_ready, UNITS * (b - 1) + 4 * m + 4)
                for s in range(SUBS):
                    for u in range(4):
                        last = nc.tensor.matmul(small_ps[DH * u:DH * (u + 1), 0:SUB], den_w[:, s * DH:(s + 1) * DH],
                                                qp[:, 1 - par, 4 * m + u, s * SUB:(s + 1) * SUB],
                                                start=s == 0, stop=s == SUBS - 1)
                last.then_inc(small_done, 1)

            def output(c, cpar, i):
                at_least(pe, proj_read, NCHUNK * c + (0, 0, 1, 3)[i])
                if isinstance(c, int) and c == B - 1:
                    pe.wait_ge(normed_last, 2 * i + 2)
                else:
                    at_least(pe, normed, UNITS * c + 2 * i + 2)
                for d in range(2):
                    last = nc.tensor.matmul(proj_ps[i][d * C:(d + 1) * C, :], mix[:, :],
                                            qp[:, cpar, 2 * i + d, :], start=True, stop=True)
                last.then_inc(proj_done, 1)

            def iteration(b, par, cur, prev, pp):
                for i in range(4):
                    if cur:
                        token_major(b, par, i)
                        keys(b, par, i)
                    if i == 0 and pp:
                        output(b - 2, par, 2)
                    if i < 2 and prev:
                        small(b, 2 * i, prev)
                    if cur and i == 3:
                        gather(b, 2)
                    if cur:
                        queries(b, par, i)
                    if i == 0 and pp:
                        output(b - 2, par, 3)
                    if cur and i in (1, 2):
                        gather(b, i - 1)
                    if i < 2 and prev:
                        denominators(b, par, i)
                    if i == 2 and pp:
                        small(b, 4, prev)
                    if i == 3 and pp:
                        small(b, 5, prev)
                    if i == 3 and prev:
                        at_least(pe, small_read, small_step(b, 2))
                        output(b - 1, 1 - par, 0)
                    if cur and i == 3:
                        gather(b, 3)
                    if i == 3 and prev:
                        at_least(pe, small_read, small_step(b, 5 if pp else 3))
                        output(b - 1, 1 - par, 1)

            batches(pe, iteration)

        @block.vector
        def _(dve):
            def row_low_part(slot, g, rows):
                gb = slice(g * GB, (g + 1) * GB)
                dve.wait_ge(row_ready[g], rows)
                nc.vector.tensor_tensor(low[:, slot, gb, HALO:HALO + J], state[:, slot, gb, :],
                                        high[:, slot, gb, HALO:HALO + J], ALU.subtract).then_inc(low_ready[g], 1)

            def start(g, rows, src):
                gb = slice(g * GB, (g + 1) * GB)
                nc.vector.tensor_copy(high[:, 0, gb, HALO:HALO + J], src).then_inc(high_ready[g], 1)
                nc.vector.tensor_copy(state[:, 0, gb, :], src).then_inc(row_ready[g], 1)
                row_low_part(0, g, rows)

            def step(u, g, rows, add, beside):
                slot = (u + 1) % SLOTS
                gb = slice(g * GB, (g + 1) * GB)
                for to, ready in ((high[:, slot, gb, HALO:HALO + J], high_ready), (state[:, slot, gb, :], row_ready)):
                    nc.vector.scalar_tensor_tensor(
                        out=to, in0=conv[g][u % SLOTS][:, 0:GB * J].rearrange("p (b j) -> p b j", b=GB), scalar=0.0, in1=add,
                        op0=ALU.max, op1=ALU.add).then_inc(ready[g], 1)
                beside(g)
                row_low_part(slot, g, rows)

            dve.wait_ge(row0_loaded, 32)
            dve.wait_ge(zeroed, 2)
            for g in range(GROUPS):
                start(g, 1, row0[:, g * GB:(g + 1) * GB, 1:1 + W:2])
            split_weights(dve, 0)

            for k in range(4):
                base = k * STEPS
                save = (1, 65, 128, 191)[k]
                rows = (1, 64, 128, 191)[k]
                if k == 2:
                    dve.wait_ge(saved, 128)
                    for g in range(GROUPS):
                        start(g, rows, cols[:, 0, g * GB:(g + 1) * GB, :])
                body = LONG_BODY if k < 3 else BODY

                def steps(n, stat=None):
                    s = n * body
                    down = n * -body + (H - 2)
                    for u in range(body):
                        if k == 0 and u % RAW_ROWS == 0:
                            dve.wait_ge(raw_loaded[u // RAW_ROWS], n * 32 + 32)
                        dve.wait_ge(saved, s + max(save + u - 2, (1, 0, 0, 190)[k]))
                        for g in range(GROUPS):
                            gb = slice(g * GB, (g + 1) * GB)
                            if k == 0:
                                r = u % RAW_ROWS
                                add = raw[:, u // RAW_ROWS, gb, 1 + r * W:1 + (r + 1) * W:2]
                            elif k == 2:
                                add = cols[:, bass.ds(s + (u + 1), 1), gb, :].rearrange("p o b j -> p (o b) j")
                            else:
                                src = rows_h if k == 1 else cols
                                add = src[:, bass.ds(down - u, 1), gb, :].rearrange("p o b j -> p (o b) j")
                            dve.wait_ge(conv_done[g], s + (base + u + 1))
                            step(u, g, s + (rows + u + 1), add,
                                 lambda g: stat(u, g) if stat is not None and u < B else None)

                if k < 3:
                    with dve.Fori(0, STEPS // body) as n:
                        steps(n)
                else:
                    steps(0)
                    with dve.Fori(1, BLOCKS) as n:
                        def stat(b, g):
                            first, count = ((0, BODY // 2), (BODY // 2, BODY - BODY // 2))[g]
                            nc.vector.bn_stats(stats[:, b, bass.ds(n * 2 + (g - 2), 1), :].rearrange("p o s -> p (o s)"),
                                               cols[:, bass.ds(n * -BODY + (W + first), count), b, :])

                        steps(n, stat)

            def link(ins, count):
                ins.then_inc(chain, 1)
                dve.wait_ge(chain, count)

            dve.wait_ge(saved, 254)
            dve.wait_ge(norm_loaded, 16 * 8)
            nc.vector.tensor_scalar(bias1[:, :], norm[:, 1:2], 1.0 / PROJ_SCALE, None, ALU.mult)
            for b in range(B):
                last = nc.vector.bn_stats(stats[:, b, 2 * BLOCKS - 2, :], cols[:, 0:W - (BLOCKS - 1) * BODY, b, :])
            link(last, 1)
            for b in range(B):
                last = nc.vector.bn_aggr(agg[:, b, :], stats[:, b, :, :].rearrange("p n s -> p (n s)"))
            last.then_inc(stat_ready, 1)
            dve.wait_ge(wt_ready, 1)
            for d in range(2):
                half_p = slice(d * C, (d + 1) * C)
                last = nc.vector.tensor_tensor(w_two_low[half_p, d], w_two[half_p], w_two_high[half_p], ALU.subtract)
            last.then_inc(wt_ready, 1)
            dve.wait_ge(stat_ready, 1)
            dve.wait_ge(stat_done, 1)
            mean1, var1 = small_ps[:, 0:B], small_ps[:, B:2 * B]
            link(nc.vector.scalar_tensor_tensor(out=dev[:, :], in0=mean1, scalar=-1.0, in1=agg[:, :, 0],
                                                op0=ALU.mult, op1=ALU.add), 2)
            link(nc.vector.tensor_tensor(dev[:, :], dev[:, :], dev[:, :], ALU.mult), 3)
            nc.vector.tensor_tensor(spread[:, :], dev[:, :], agg[:, :, 1], ALU.add).then_inc(stat_ready, 1)
            dve.wait_ge(stat_done, 2)
            nc.vector.tensor_scalar(dev[:, :], var1, EPS_GN, None, ALU.add).then_inc(var_ready, 1)
            dve.wait_ge(scale_ready, 2)
            link(nc.vector.scalar_tensor_tensor(out=shift1[:, :], in0=mean1, scalar=-1.0, in1=scale1[:, :],
                                                op0=ALU.mult, op1=ALU.mult), 4)
            link(nc.vector.tensor_scalar(shift1[:, :], shift1[:, :], bias1[:, :], None, ALU.add), 5)

            def normalise(b, par):
                at_least(dve, query_done, UNITS * (b - 1))
                one = lambda v: v[:, bass.ds(b, 1)]
                nc.vector.tensor_scalar(yn[:, par, :].rearrange("p (w j) -> p w j", j=J),
                                        cols[:, :, bass.ds(b, 1), :].rearrange("p w o j -> p w (o j)"),
                                        one(scale1), one(shift1), ALU.mult, ALU.add).then_inc(yn_ready, 1)

            def keys(b, i):
                for m in (2 * i, 2 * i + 1):
                    at_least(dve, key_exp, KBANKS * b + m + 1)
                    at_least(dve, acc_used, 4 * b + m // 2 - 1)
                    nc.vector.scalar_tensor_tensor(out=kp[:, m % 4, :], in0=ex[:, m % 2, :], scalar=1.0,
                                                   in1=key_ps[m % 2][:, :], op0=ALU.min, op1=ALU.max)\
                        .then_inc(kp_ready, 1)

            def queries(b, par, i):
                for u in (2 * i, 2 * i + 1):
                    at_least(dve, query_read, UNITS * b + u + 1)
                    at_least(dve, proj_done, NCHUNK * (b - 2) + i + 1)
                    nc.vector.scalar_tensor_tensor(out=qp[:, par, u, :], in0=ex[:, 2 + u % 2, :], scalar=1.0,
                                                   in1=re[:, u % 2, :], op0=ALU.min, op1=ALU.add).then_inc(qp_ready, 1)

            def small(b, n):
                at_least(dve, small_done, small_step(b, n))
                if n == 0:
                    nc.vector.tensor_scalar(den_w[:, :], head_of, small_ps[:, 0:1], None, ALU.mult)
                    nc.vector.tensor_tensor(kv[:, :], small_ps[:, P:2 * P], same_head, ALU.mult).then_inc(small_read, 1)
                if n == 2:
                    nc.vector.tensor_copy(mix[:, :], small_ps[:, 0:C]).then_inc(small_read, 1)
                if n == 4:
                    at_least(dve, affine_ready, b - 1)
                    mean2 = small_ps[:, 0:1]
                    nc.vector.tensor_scalar(dev2[:, 3:4], mean2, -1.0, None, ALU.mult)
                    nc.vector.scalar_tensor_tensor(out=dev2[:, 0:1], in0=mean2, scalar=-1.0, in1=agg2[:, 0:1],
                                                   op0=ALU.mult, op1=ALU.add).then_inc(small_read, 1)
                    at_least(dve, small_read, small_step(b, n))
                    nc.vector.tensor_scalar(dev2[:, 2:3], dev2[:, 0:1], dev2[:, 0:1], agg2[:, 1:2],
                                            ALU.mult, ALU.add).then_inc(stat_ready, 1)
                if n == 5:
                    nc.vector.tensor_scalar(dev2[:, 1:2], small_ps[:, 0:1], EPS_GN, None, ALU.add)\
                        .then_inc(small_read, 1)
                if n in (1, 3):
                    m = n // 2
                    at_least(dve, recip_ready, 2 * (b - 1) + m)
                    nc.vector.tensor_scalar(den[:, :], small_ps[:, 0:SUB], EPS_ATTN, None, ALU.add).then_inc(small_read, 1)
                    at_least(dve, small_read, small_step(b, n))
                    at_least(dve, bounced, 16 * (2 * (b - 2) + m + 1))
                    nc.vector.reciprocal(recip[:, m, :], den[:, :]).then_inc(recip_ready, 1)

            def output_stats(b, par, prev):
                for i in range(NCHUNK):
                    if i == 0 or not prev:
                        at_least(dve, proj_read, NCHUNK * (b - 1) if prev else NCHUNK * (b - 2) + i + 1)
                    last = nc.vector.bn_stats(stats2[:, i, :], proj[:, par, i * CHUNK:(i + 1) * CHUNK])
                last.then_inc(norm2, 1)
                at_least(dve, norm2, b - 1)
                settled(dve)
                nc.vector.bn_aggr(agg2[:, :], stats2[:, :, :].rearrange("p n s -> p (n s)")).then_inc(stat_ready, 1)

            def iteration(b, par, cur, prev, pp):
                for i in range(4):
                    if i == 3 and pp:
                        small(b, 4)
                    if cur:
                        keys(b, i)
                    if i < 2 and prev:
                        small(b, 2 * i)
                    if i == 3 and has_next(b, cur):
                        low_of(dve, b + 1, 1 - par, 1, low_part)
                    if i == 3 and pp:
                        small(b, 5)
                    if cur:
                        queries(b, par, i)
                    if i < 2 and prev:
                        small(b, 2 * i + 1)
                    if i == 1 and pp:
                        output_stats(b, par, prev)
                    if i == 0 and has_next(b, cur):
                        normalise(b + 1, 1 - par)
                    if i == 2 and has_next(b, cur):
                        low_of(dve, b + 1, 1 - par, 0, low_part)
                if prev and not cur:
                    last_normalised(b, par)
                if pp and not prev:
                    last_residual(b, par)

            def last_normalised(b, par):
                for u in range(UNITS):
                    if u % 4 == 0:
                        dve.wait_ge(recip_sent[u // 4], 64 * b)
                    nc.vector.tensor_tensor(qp[:, 1 - par, u, :], qp[:, 1 - par, u, :], recip_b[:, u, :],
                                            ALU.mult).then_inc(normed_last, 1)

            def last_residual(b, par):
                for h, rows in enumerate(HALVES):
                    dve.wait_ge(affine_done, b - 1 + h)
                    nc.vector.tensor_tensor(
                        fin_last[:, rows, :].rearrange("p j w -> p w j"),
                        proj[:, par, :].rearrange("p (w j) -> p w j", j=J)[:, :, rows],
                        cols[:, :, b - 2, rows], ALU.add).then_inc(fin_ready, 1)

            for i in range(NCHUNK):
                w = slice(i * CHUNK // J, (i + 1) * CHUNK // J)
                nc.vector.tensor_scalar(yn[:, 0, i * CHUNK:(i + 1) * CHUNK].rearrange("p (w j) -> p w j", j=J),
                                        cols[:, w, 0, :], scale1[:, 0:1], shift1[:, 0:1], ALU.mult, ALU.add)\
                    .then_inc(yn_ready if i == NCHUNK - 1 else first_yn, 1)
                for d in range(2):
                    here, there, n = slice(d * C, (d + 1) * C), slice((1 - d) * C, (2 - d) * C), chunk_of(i)
                    if i == NCHUNK - 1:
                        dve.wait_ge(high_part, d + 1)
                    else:
                        dve.wait_ge(first_high, 2 * i + d + 1)
                    nc.vector.tensor_tensor(stacked[there, 0, d, n], yn[here, 0, n], stacked[here, 0, d, n],
                                            ALU.subtract).then_inc(low_part if i == NCHUNK - 1 else first_low, 1)
            batches(dve, iteration)

        @block.scalar
        def _(act):
            def down(slot, n, between=lambda: None):
                for g in range(GROUPS):
                    gb = slice(g * GB, (g + 1) * GB)
                    act.wait_ge(high_ready[g], n)
                    act.activation(high_down[:, slot, gb, HALO:HALO + J], high[:, slot, gb, HALO:HALO + J], ACT.Copy,
                                   scale=1.0 / LOW_SCALE).then_inc(down_ready[g], 1)
                    if g == 0:
                        between()
                for g in range(GROUPS):
                    act.wait_ge(row_ready[g], n)

            def save(slot, to):
                act.activation(to, state[:, slot, :, :], ACT.Copy).then_inc(saved, 1)

            def scatter(pw, u, n=0):
                ph, jh = u % 2, n * -3 + (H // 2 - 1 - (u + 1) // 2)
                dst = cols_w[ph * C:(ph + 1) * C, :].rearrange("p (w two b j) -> p w two b j", two=2, b=B, j=J)
                dst = dst[:, :, pw, :, bass.ds(jh, 1)].rearrange("p w b o -> p (o b) w")
                s = act.activation(dst, state[pw * C:(pw + 1) * C, (u + 1) % SLOTS, :, :], ACT.Copy)
                if pw == 1:
                    s.then_inc(saved, 1)

            down(0, 1)
            save(0, rows_h[:, 0])
            with act.Fori(0, STEPS - BODY + 1, BODY) as s:
                for u in range(BODY):
                    down((u + 1) % SLOTS, s + (u + 2))
                    save((u + 1) % SLOTS, rows_h[:, bass.ds(s + (u + 1), 1), :, :].rearrange("p o b j -> p (o b) j"))
            scatter(0, -1)
            with act.Fori(0, STEPS // 6) as n:
                for u in range(6):
                    down((u + 1) % SLOTS, n * 6 + (65 + u), lambda: scatter(1, u - 1, n=n))
                    scatter(0, u, n=n)
            for u in range(STEPS - STEPS % 6, STEPS):
                down((u + 1) % SLOTS, 65 + u, lambda: scatter(1, u - 1))
                scatter(0, u)
            scatter(1, STEPS - 1)
            down(0, 128)
            for k, rows in ((2, 129), (3, 192)):
                with act.Fori(0, STEPS // BODY) as n:
                    for u in range(BODY):
                        down((u + 1) % SLOTS, n * BODY + (rows + u))
                        w = n * BODY + (u + 1) if k == 2 else n * -BODY + (W - 2 - u)
                        save((u + 1) % SLOTS, cols[:, bass.ds(w, 1), :, :].rearrange("p o b j -> p (o b) j"))

            act.wait_ge(wt_done, 1)
            act.activation(w_two[:, :, :].rearrange("p q n -> p (q n)"), tok_ps[:, 0:2 * P], ACT.Copy, scale=PROJ_SCALE)
            act.activation(w_two_high[:, :, :].rearrange("p q n -> p (q n)"), tok_ps[:, 0:2 * P], ACT.Copy,
                           scale=PROJ_SCALE)
            act.activation(w_v[:, :], tok_ps[:, 2 * P:3 * P], ACT.Copy, scale=PROJ_SCALE)
            for d in range(2):
                half_p = slice(d * C, (d + 1) * C)
                act.activation(two_idents[half_p, :], ident[half_p, half_p], ACT.Copy)
            act.activation(w_o[:, :], acc_ps[:, 0:C], ACT.Copy).then_inc(wt_ready, 1)

            def high_of(b, par, d):
                if d == 0:
                    at_least(act, yn_ready, b + 1)
                half_p = slice(d * C, (d + 1) * C)
                act.activation(stacked[half_p, par, d], yn[half_p, par], ACT.Copy).then_inc(high_part, 1)

            def tokens(b, i):
                at_least(act, tok_done, 4 * b + i + 1)
                at_least(act, acc_used, 4 * b + i - 1)
                act.activation(tok[:, i % 2, :], tok_ps[:, :], ACT.Copy).then_inc(tok_ready, 1)

            def gathered(b):
                at_least(act, acc_used, 4 * b)
                at_least(act, small_read, small_step(b, 0) - 1)
                act.activation(acc_g[:, :], acc_ps[:, 0:P], ACT.Copy)
                act.activation(acc_s[:, :], acc_ps[:, P:3 * P], ACT.Copy).then_inc(acc_read, 1)

            def collect(c, cpar, chunks):
                for i in chunks:
                    at_least(act, proj_done, NCHUNK * c + i + 1)
                    if i == 0:
                        at_least(act, fin_ready, c)
                    act.activation(proj[:, cpar, i * CHUNK:(i + 1) * CHUNK], proj_ps[i][:, :], ACT.Copy)\
                       .then_inc(proj_read, 1)

            def iteration(b, par, cur, prev, pp):
                for i in range(4):
                    if i == 0 and prev:
                        gathered(b)
                    if cur:
                        tokens(b, i)
                        for m in (2 * i, 2 * i + 1):
                            at_least(act, key_done, KBANKS * b + m + 1)
                            at_least(act, kp_ready, KBANKS * b + m - 1)
                            act.activation(ex[:, m % 2, :], key_ps[m % 2][:, :], ACT.Exp, bias=minus_one[:, :])\
                               .then_inc(key_exp, 1)
                    if i == 0 and pp:
                        collect(b - 2, par, (2,))
                    if cur:
                        for u in (2 * i, 2 * i + 1):
                            at_least(act, query_done, UNITS * b + u + 1)
                            at_least(act, qp_ready, UNITS * b + u - 1)
                            act.activation(ex[:, 2 + u % 2, :], query_ps[u % 2][:, :], ACT.Exp)
                            act.activation(re[:, u % 2, :], query_ps[u % 2][:, :], ACT.Relu).then_inc(query_read, 1)
                    if i == 0 and pp:
                        collect(b - 2, par, (3,))
                    if i in (1, 2) and has_next(b, cur):
                        high_of(b + 1, 1 - par, i - 1)
                if cur and prev:
                    collect(b - 1, 1 - par, (0, 1))
                if pp:
                    at_least(act, affine_ready, b)
                    for rows in (slice(0, J),) if prev else HALVES:
                        part_o = proj[:, par, :].rearrange("p (w j) -> p w j", j=J)[:, :, rows]
                        act.activation(part_o, part_o, ACT.Identity, bias=shift2[:, par:par + 1],
                                       scale=scale2[:, par:par + 1]).then_inc(affine_done, 1)
                if prev and not cur:
                    collect(b - 1, 1 - par, (0, 1))

            for i in range(NCHUNK):
                act.wait_ge(*((yn_ready, 1) if i == NCHUNK - 1 else (first_yn, i + 1)))
                for d in range(2):
                    half_p = slice(d * C, (d + 1) * C)
                    act.activation(stacked[half_p, 0, d, chunk_of(i)], yn[half_p, 0, chunk_of(i)], ACT.Copy)\
                       .then_inc(high_part if i == NCHUNK - 1 else first_high, 1)
            batches(act, iteration)


_INS = ["x", "L0_conv_k_td", "L0_conv_k_dt", "L0_conv_k_lr", "L0_conv_k_rl", "L1_conv_gn1_w", "L1_conv_gn1_b",
        "L1_conv_w_qkv", "L1_conv_w_out", "L1_conv_gn2_w", "L1_conv_gn2_b"]


def kernel(**inputs):
    import concourse.bacc as bacc
    from concourse.bass_utils import run_bass_kernel_spmd

    nc = bacc.Bacc("TRN2", target_bir_lowering=False, num_devices=1)
    arrays = {name: np.ascontiguousarray(inputs[name]) for name in _INS}
    arrays["consts"] = constants()
    args = [nc.dram_tensor(name, a.shape, mybir.dt.from_np(a.dtype), kind="ExternalInput").ap()
            for name, a in arrays.items()]
    args.append(nc.dram_tensor("out", (B, C, H, W), F32, kind="ExternalOutput").ap())
    build(nc, *args)
    r = run_bass_kernel_spmd(nc, [arrays], core_ids=[0])
    return r.results[0]["out"]
```
